# Optimizing a Trainium2 kernel written in Bass

```python
import numpy as np
import jax
import jax.numpy as jnp

def _softmax(x, axis=-1):
    return jax.nn.softmax(x, axis=axis)

def _gelu(x):
    return jax.nn.gelu(x, approximate=True)

def _silu(x):
    return jax.nn.silu(x)

def _sigmoid(x):
    return jax.nn.sigmoid(x)

def _layernorm(x, axis=-1, eps=1e-05):
    m = jnp.mean(x, axis=axis, keepdims=True)
    v = jnp.var(x, axis=axis, keepdims=True)
    return (x - m) / jnp.sqrt(v + eps)

def _scatter_add(tgt, idx, src, axis=0):
    return tgt.at[idx].add(src)

def _segment_sum(src, seg, n):
    return jax.ops.segment_sum(src, seg, n)
kernel_name = 'mk_macaron_d1_jaxref_r8_033e99'

def setup_inputs(seed: int=0):
    np.random.seed(seed)
    _w = jnp.asarray

    def _L0_attn_setup():
        import jax, jax.numpy as jnp
        import numpy as np
        D_MODEL = 128
        D_STATE = 16
        EXPAND = 2
        D_HEAD = 64
        D_CONV = 4
        FFN = 352
        NORMALIZE_BC = True
        D_INNER = EXPAND * D_MODEL
        N_HEADS = D_INNER // D_HEAD
        EPS = 1e-06

        def _rmsnorm(x, w):
            v = jnp.mean(x * x, axis=-1, keepdims=True)
            return x * jax.lax.rsqrt(v + EPS) * w

        def _mixer(x, in_proj_w, conv_w, conv_b, A_log, dt_bias, D, out_proj_w):
            b, l, _ = x.shape
            zxbcdt = x @ in_proj_w.T
            z, xBC, dt_raw = jnp.split(zxbcdt, [D_INNER, 2 * D_INNER + 2 * D_STATE], axis=-1)
            xp = jnp.pad(xBC, ((0, 0), (D_CONV - 1, 0), (0, 0)))
            y = conv_b + sum((xp[:, k:k + l, :] * conv_w[:, k] for k in range(D_CONV)))
            xBC = jax.nn.silu(y)
            u, Bm, Cm = jnp.split(xBC, [D_INNER, D_INNER + D_STATE], axis=-1)
            if NORMALIZE_BC:
                Bm = Bm / (jnp.linalg.norm(Bm, axis=-1, keepdims=True) + EPS)
                Cm = Cm / (jnp.linalg.norm(Cm, axis=-1, keepdims=True) + EPS)
            dt = jax.nn.softplus(dt_raw + dt_bias)
            A = jnp.exp(A_log)
            u = u.reshape(b, l, N_HEADS, D_HEAD)

            def step(carry, inp):
                w, ys = carry
                dt_t, B_t, C_t, u_t = inp
                S = 1.0 / (1.0 + dt_t[:, :, None] ** 2 * A[None])
                Sb = S[:, :, None, :]
                dtb = dt_t[:, :, None, None]
                Ab = A[None, :, None, :]
                Bu = B_t[:, None, None, :] * u_t[..., None]
                w = Sb * (w - dtb * Ab * ys + dtb * Bu)
                ys = ys + dtb * w
                o = jnp.einsum('bhdn,bn->bhd', ys, C_t)
                return ((w, ys), o)
            init = (jnp.zeros((b, N_HEADS, D_HEAD, D_STATE), x.dtype), jnp.zeros((b, N_HEADS, D_HEAD, D_STATE), x.dtype))
            xs = (dt.transpose(1, 0, 2), Bm.transpose(1, 0, 2), Cm.transpose(1, 0, 2), u.transpose(1, 0, 2, 3))
            _, ys = jax.lax.scan(step, init, xs)
            ys = ys.transpose(1, 0, 2, 3) + D[None, None, :, None] * u
            out = ys.reshape(b, l, D_INNER) * jax.nn.silu(z)
            return out @ out_proj_w.T
        key = jax.random.key(seed)
        ks = jax.random.split(key, 12)
        B, L = (4, 256)
        proj_dim = 2 * D_INNER + 2 * D_STATE + N_HEADS
        conv_ch = D_INNER + 2 * D_STATE
        s = lambda k, shape, sc: jax.random.normal(k, shape, jnp.float32) * sc
        return {'x': s(ks[0], (B, L, D_MODEL), 1.0), 'norm1_w': jnp.ones((D_MODEL,), jnp.float32), 'in_proj_w': s(ks[1], (proj_dim, D_MODEL), D_MODEL ** (-0.5)), 'conv_w': s(ks[2], (conv_ch, D_CONV), 0.3), 'conv_b': jnp.zeros((conv_ch,), jnp.float32), 'A_log': s(ks[3], (N_HEADS, D_STATE), 0.5), 'dt_bias': s(ks[4], (N_HEADS,), 0.5), 'D': s(ks[5], (N_HEADS,), 1.0), 'out_proj_w': s(ks[6], (D_MODEL, D_INNER), D_INNER ** (-0.5)), 'norm2_w': jnp.ones((D_MODEL,), jnp.float32), 'gate_w': s(ks[7], (FFN, D_MODEL), D_MODEL ** (-0.5)), 'up_w': s(ks[8], (FFN, D_MODEL), D_MODEL ** (-0.5)), 'down_w': s(ks[9], (D_MODEL, FFN), FFN ** (-0.5))}
    _L0_attn_in = _L0_attn_setup()

    def _L0_ffn_setup():
        import jax, jax.numpy as jnp
        import numpy as np
        D_MODEL = 128
        HIDDEN = 256
        N_EXPERTS = 8
        TOP_K = 2
        key = jax.random.key(seed)
        ks = jax.random.split(key, 9)
        s = 0.02
        x = jax.random.normal(ks[0], (4, 256, D_MODEL), dtype=jnp.float32)
        sw1 = jax.random.normal(ks[1], (D_MODEL, HIDDEN), dtype=jnp.float32) * s
        sw2 = jax.random.normal(ks[2], (D_MODEL, HIDDEN), dtype=jnp.float32) * s
        sw3 = jax.random.normal(ks[3], (HIDDEN, D_MODEL), dtype=jnp.float32) * s
        ew1 = jax.random.normal(ks[4], (N_EXPERTS, D_MODEL, HIDDEN), dtype=jnp.float32) * s
        ew2 = jax.random.normal(ks[5], (N_EXPERTS, D_MODEL, HIDDEN), dtype=jnp.float32) * s
        ew3 = jax.random.normal(ks[6], (N_EXPERTS, HIDDEN, D_MODEL), dtype=jnp.float32) * s
        rw = jax.random.normal(ks[7], (D_MODEL, N_EXPERTS), dtype=jnp.float32) * s
        rb = jax.random.normal(ks[8], (N_EXPERTS,), dtype=jnp.float32) * s
        return {'x': x, 'sw1': sw1, 'sw2': sw2, 'sw3': sw3, 'ew1': ew1, 'ew2': ew2, 'ew3': ew3, 'rw': rw, 'rb': rb}
    _L0_ffn_in = _L0_ffn_setup()
    _d = {'L0_attn_x': _L0_attn_in['x'], 'L0_attn_norm1_w': _L0_attn_in['norm1_w'], 'L0_attn_in_proj_w': _L0_attn_in['in_proj_w'], 'L0_attn_conv_w': _L0_attn_in['conv_w'], 'L0_attn_conv_b': _L0_attn_in['conv_b'], 'L0_attn_A_log': _L0_attn_in['A_log'], 'L0_attn_dt_bias': _L0_attn_in['dt_bias'], 'L0_attn_D': _L0_attn_in['D'], 'L0_attn_out_proj_w': _L0_attn_in['out_proj_w'], 'L0_attn_norm2_w': _L0_attn_in['norm2_w'], 'L0_attn_gate_w': _L0_attn_in['gate_w'], 'L0_attn_up_w': _L0_attn_in['up_w'], 'L0_attn_down_w': _L0_attn_in['down_w'], 'L0_ffn_sw1': _L0_ffn_in['sw1'], 'L0_ffn_sw2': _L0_ffn_in['sw2'], 'L0_ffn_sw3': _L0_ffn_in['sw3'], 'L0_ffn_ew1': _L0_ffn_in['ew1'], 'L0_ffn_ew2': _L0_ffn_in['ew2'], 'L0_ffn_ew3': _L0_ffn_in['ew3'], 'L0_ffn_rw': _L0_ffn_in['rw'], 'L0_ffn_rb': _L0_ffn_in['rb']}
    _x0 = _d['L0_attn_x']
    _d['L0_attn_x'] = jax.random.normal(jax.random.fold_in(jax.random.key(seed), 1), (4, 1024, 128), dtype=_x0.dtype)
    del _x0
    return _d

def reference(L0_attn_x, L0_attn_norm1_w, L0_attn_in_proj_w, L0_attn_conv_w, L0_attn_conv_b, L0_attn_A_log, L0_attn_dt_bias, L0_attn_D, L0_attn_out_proj_w, L0_attn_norm2_w, L0_attn_gate_w, L0_attn_up_w, L0_attn_down_w, L0_ffn_sw1, L0_ffn_sw2, L0_ffn_sw3, L0_ffn_ew1, L0_ffn_ew2, L0_ffn_ew3, L0_ffn_rw, L0_ffn_rb):

    def _L0_attn_ref(x, norm1_w, in_proj_w, conv_w, conv_b, A_log, dt_bias, D, out_proj_w, norm2_w, gate_w, up_w, down_w):
        import jax, jax.numpy as jnp
        import numpy as np
        D_MODEL = 128
        D_STATE = 16
        EXPAND = 2
        D_HEAD = 64
        D_CONV = 4
        FFN = 352
        NORMALIZE_BC = True
        D_INNER = EXPAND * D_MODEL
        N_HEADS = D_INNER // D_HEAD
        EPS = 1e-06

        def _rmsnorm(x, w):
            v = jnp.mean(x * x, axis=-1, keepdims=True)
            return x * jax.lax.rsqrt(v + EPS) * w

        def _mixer(x, in_proj_w, conv_w, conv_b, A_log, dt_bias, D, out_proj_w):
            b, l, _ = x.shape
            zxbcdt = x @ in_proj_w.T
            z, xBC, dt_raw = jnp.split(zxbcdt, [D_INNER, 2 * D_INNER + 2 * D_STATE], axis=-1)
            xp = jnp.pad(xBC, ((0, 0), (D_CONV - 1, 0), (0, 0)))
            y = conv_b + sum((xp[:, k:k + l, :] * conv_w[:, k] for k in range(D_CONV)))
            xBC = jax.nn.silu(y)
            u, Bm, Cm = jnp.split(xBC, [D_INNER, D_INNER + D_STATE], axis=-1)
            if NORMALIZE_BC:
                Bm = Bm / (jnp.linalg.norm(Bm, axis=-1, keepdims=True) + EPS)
                Cm = Cm / (jnp.linalg.norm(Cm, axis=-1, keepdims=True) + EPS)
            dt = jax.nn.softplus(dt_raw + dt_bias)
            A = jnp.exp(A_log)
            u = u.reshape(b, l, N_HEADS, D_HEAD)

            def step(carry, inp):
                w, ys = carry
                dt_t, B_t, C_t, u_t = inp
                S = 1.0 / (1.0 + dt_t[:, :, None] ** 2 * A[None])
                Sb = S[:, :, None, :]
                dtb = dt_t[:, :, None, None]
                Ab = A[None, :, None, :]
                Bu = B_t[:, None, None, :] * u_t[..., None]
                w = Sb * (w - dtb * Ab * ys + dtb * Bu)
                ys = ys + dtb * w
                o = jnp.einsum('bhdn,bn->bhd', ys, C_t)
                return ((w, ys), o)
            init = (jnp.zeros((b, N_HEADS, D_HEAD, D_STATE), x.dtype), jnp.zeros((b, N_HEADS, D_HEAD, D_STATE), x.dtype))
            xs = (dt.transpose(1, 0, 2), Bm.transpose(1, 0, 2), Cm.transpose(1, 0, 2), u.transpose(1, 0, 2, 3))
            _, ys = jax.lax.scan(step, init, xs)
            ys = ys.transpose(1, 0, 2, 3) + D[None, None, :, None] * u
            out = ys.reshape(b, l, D_INNER) * jax.nn.silu(z)
            return out @ out_proj_w.T
        h = x + _mixer(_rmsnorm(x, norm1_w), in_proj_w, conv_w, conv_b, A_log, dt_bias, D, out_proj_w)
        hn = _rmsnorm(h, norm2_w)
        ffn = jax.nn.silu(hn @ gate_w.T) * (hn @ up_w.T) @ down_w.T
        return h + ffn

    def _L0_ffn_ref(x, sw1, sw2, sw3, ew1, ew2, ew3, rw, rb):
        import jax, jax.numpy as jnp
        import numpy as np
        D_MODEL = 128
        HIDDEN = 256
        N_EXPERTS = 8
        TOP_K = 2
        shared = jnp.einsum('bth,hd->btd', jax.nn.silu(jnp.einsum('btd,dh->bth', x, sw1)) * jnp.einsum('btd,dh->bth', x, sw2), sw3)
        probs = jax.nn.softmax(jnp.einsum('btd,de->bte', x, rw) + rb, axis=-1)
        w, idx = jax.lax.top_k(probs, TOP_K)
        w = w / jnp.sum(w, axis=-1, keepdims=True)
        gates = jnp.sum(w[..., None] * jax.nn.one_hot(idx, N_EXPERTS, dtype=x.dtype), axis=-2)
        h = jax.nn.silu(jnp.einsum('btd,edh->beth', x, ew1)) * jnp.einsum('btd,edh->beth', x, ew2)
        eout = jnp.einsum('beth,ehd->betd', h, ew3)
        routed = jnp.einsum('betd,bte->btd', eout, gates)
        return shared + routed
    x = L0_attn_x
    x = x + 0.5 * _L0_ffn_ref(_layernorm(x, axis=-1), L0_ffn_sw1, L0_ffn_sw2, L0_ffn_sw3, L0_ffn_ew1, L0_ffn_ew2, L0_ffn_ew3, L0_ffn_rw, L0_ffn_rb)
    x = x + _L0_attn_ref(_layernorm(x, axis=-1), L0_attn_norm1_w, L0_attn_in_proj_w, L0_attn_conv_w, L0_attn_conv_b, L0_attn_A_log, L0_attn_dt_bias, L0_attn_D, L0_attn_out_proj_w, L0_attn_norm2_w, L0_attn_gate_w, L0_attn_up_w, L0_attn_down_w)
    x = x + 0.5 * _L0_ffn_ref(_layernorm(x, axis=-1), L0_ffn_sw1, L0_ffn_sw2, L0_ffn_sw3, L0_ffn_ew1, L0_ffn_ew2, L0_ffn_ew3, L0_ffn_rw, L0_ffn_rb)
    return x

_drawn_inputs = setup_inputs


def setup_inputs(seed=0):
    import zlib

    import numpy as np

    out = dict(_drawn_inputs(seed))
    spreads = {'L0_attn_norm1_w': (1.0, 0.2),
     'L0_attn_conv_b': (0.0, 0.313),
     'L0_attn_norm2_w': (1.0, 0.2)}
    factors = {'L0_attn_dt_bias': 5.687,
     'L0_ffn_sw1': 8.0,
     'L0_ffn_sw2': 8.0,
     'L0_ffn_sw3': 8.0,
     'L0_ffn_ew1': 8.0,
     'L0_ffn_ew2': 8.0,
     'L0_ffn_ew3': 8.0,
     'L0_ffn_rw': 8.0,
     'L0_ffn_rb': 8.0}
    for name, (base, spread) in spreads.items():
        noise = np.random.default_rng([zlib.crc32(name.encode()), seed]).standard_normal(out[name].shape)
        drawn = base * np.exp(spread * noise) if base else spread * noise
        out[name] = jnp.asarray(drawn.astype(out[name].dtype))
    for name, factor in factors.items():
        out[name] = (out[name] * factor).astype(out[name].dtype)
    return out
```

```python
import numpy as np
import concourse.bass as bass
from concourse import mybir
from contextlib import ExitStack

F32 = mybir.dt.float32
F32R = mybir.dt.float32r
U32 = mybir.dt.uint32
I16 = mybir.dt.int16
BF16 = mybir.dt.bfloat16
ALU = mybir.AluOpType
ACT = mybir.ActivationFunctionType

P = 128
TOK = 4096
BT = 512
NB = TOK // BT
TT = BT // P
HID = 256
NE = 8
NX = NE + 1
STEPS = 2 * NX
LAG = 2
LN_EPS = 1e-5

NSEQ = 4
SEQ = TOK // NSEQ
ST = SEQ // P
SQ = SEQ // BT
DI = 256
NH = 4
DH = DI // NH
DS = 16
TAPS = 4
CH = 32
CT = P // CH
CS = SEQ // CH
FF = 352
FC = 3
RMS_EPS = 1e-6
ROUND = 1.5 * 2 ** 23
TWO_PI = 6.283185
CLAMP = 160.0
C_NORM1, C_NORM2, C_CONVB, C_CONVBC, C_ALOG, C_DTB, C_D, C_OFFC, C_OFFB = 0, 1, 2, 4, 5, 6, 7, 9, 10
NCOL = 11
ARENA = 22340


class Steps:

    def __init__(self, eng, sem, per, turn):
        self.eng, self.sem, self.per, self.turn, self.k = eng, sem, per, turn, 0

    def step(self, instruction):
        self.k += 1
        instruction.then_inc(self.sem, 1)

    def settle(self):
        self.eng.wait_ge(self.sem, self.turn * self.per + self.k)

    def close(self):
        assert self.k == self.per, (self.k, self.per)


def macaron(nc, A, out):
    ctx = ExitStack()
    with ctx:
        def sb(name, shape, dt=F32):
            return ctx.enter_context(nc.sbuf_tensor(name, shape, dt))

        def ps(name, shape):
            return ctx.enter_context(nc.psum_tensor(name, shape, F32))

        def sem(name):
            return ctx.enter_context(nc.semaphore(name))

        x = sb("x", [P, TOK // P, P])
        ident = sb("ident", [P, P])
        arena = sb("arena", [P, ARENA])
        used = [0, 0]

        def part(phase, shape):
            size = int(np.prod(shape[1:]))
            view = arena[0:shape[0], used[phase]:used[phase] + size]
            used[phase] += size
            assert used[phase] <= ARENA, used
            if len(shape) == 3:
                view = view.rearrange("p (a b) -> p a b", a=shape[1])
            if len(shape) == 4:
                view = view.rearrange("p (a b c) -> p a b c", a=shape[1], b=shape[2])
            return view

        w_raw = part(0, [P, NX, 2 * HID + 2 * P])
        up_hi = sb("up_hi", [P, NX, 2 * HID], F32R)
        up_lo = sb("up_lo", [P, NX, 2 * HID], F32R)
        down_hi = sb("down_hi", [P, NX, 2 * P], F32R)
        down_lo = sb("down_lo", [P, NX, 2 * P], F32R)
        rw = sb("rw", [P, NE])
        rb = sb("rb", [P, TT, NE])
        iota = sb("expert_iota", [P, TT, NE])
        pick_f = part(0, [2 * NE, NE, P])
        pick = sb("pick", [2 * NE, NE, P], F32R)
        minus_half = sb("minus_half", [P, TT])
        stats = sb("stats", [P, TT, 6])
        mv = sb("mv", [P, TT, 2])
        var_eps = sb("var_eps", [P, TT])
        rstd = sb("rstd", [P, TT])
        xn = part(0, [P, TT, P])
        xt = part(0, [P, BT])
        xt_hi = sb("xt_hi", [P, 2 * BT], F32R)
        xt_lo = sb("xt_lo", [P, 2 * BT], F32R)
        logits = sb("logits", [P, TT, NE])
        top = sb("top", [P, TT, 8])
        top_i = sb("top_i", [P, TT, 8], U32)
        top_f = sb("top_f", [P, TT, 2])
        gap = sb("gap", [P, TT])
        gap_tanh = sb("gap_tanh", [P, TT])
        share = sb("share", [P, 2, TT])
        hot = sb("hot", [P, 2, TT, NE])
        gate = sb("gate", [P, TT, NE])
        gate_parts = sb("gate_parts", [P, TT, 2 * NE])
        gates_t = sb("gates_t", [2 * NE, 2 * BT], F32R)
        silu_a = part(0, [P, 2, BT])
        gated = part(0, [P, 2, BT])
        hid = part(0, [P, 2, BT])
        hid_hi = sb("hid_hi", [P, 3, BT], F32R)
        hid_lo = sb("hid_lo", [P, 3, BT], F32R)
        half_out = part(0, [P, BT])

        ps_a = ps("ps_a", [P, 2, BT])
        ps_b = ps("ps_b", [P, 2, BT])
        ps_go = ps("ps_go", [P, 2, BT])
        ps_tr = ps("ps_tr", [P, 2, BT])
        ps_g, ps_o = ps_go[:, 0, :], ps_go[:, 1, :]
        ps_t, ps_r = ps_tr[:, 0, :], ps_tr[:, 1, :]

        col = sb("col", [P, NCOL])
        root_a = sb("root_a", [P, 1])
        root_a_inv = sb("root_a_inv", [P, 1])
        pow_in = sb("pow_in", [P, 3])
        w_tap = part(1, [P, TAPS, DI + 2 * DS])
        w_z = part(1, [P, DI])
        w_dt = part(1, [P, P])
        w_out = part(1, [P, 2, P])
        w_gate = part(1, [P, FF])
        w_up = part(1, [P, FF])
        w_down = part(1, [P, FC, P])
        restart = sb("restart", [P, CS, CH], BF16)
        restart_small = sb("restart_small", [P, ST, CT])
        causal = sb("causal", [P, CT, NH, CH], BF16)
        own_head = sb("own_head", [P, DI])
        zt = part(1, [P, TAPS - 1 + SEQ])
        us = part(1, [P, 2, SEQ])
        zs = part(1, [P, 2, SEQ])
        
        t_all = part(1, [P, 6, SEQ])
        t0, t1, t2, t3, t4, t5 = (t_all[:, n, :] for n in range(6))
        bc_rep = t_all[:, 4:6, :].rearrange("p a (g r n) -> p (a g) r n", r=2 * NH, n=DS)
        bc_act = t5[0:2 * DS, :]
        bf = part(1, [P, ST, CT * P])
        cfx = part(1, [P, ST, CT * NH * CH])
        cfs = zt[:, TAPS - 1:]
        state = sb("state", [P, 2, DI])
        state_new = sb("state_new", [P, DI])
        tm = sb("tm", [P, 2, DI + P])
        gram = sb("gram", [P, 2, CT, NH, CH])
        amv = sb("amv", [P, ST, 2])
        astats = sb("astats", [P, ST, 6])
        arstd = sb("arstd", [P, ST])
        azr = sb("azr", [P, ST])
        asmall = sb("asmall", [P, 4, ST])
        minus_half8 = sb("minus_half8", [P, ST])
        half16 = sb("half16", [P, 2 * ST])
        bc_tm = sb("bc_tm", [P, 2 * ST, DS])
        bc_sq = sb("bc_sq", [P, 2 * ST, DS])
        bc_n = sb("bc_n", [P, 3, 2 * ST])
        ctot = sb("ctot", [P, ST, CT])
        cmid = sb("cmid", [P, ST, CT])
        cinc = sb("cinc", [P, ST, CT])
        refs = sb("refs", [P, ST, CT])
        decay = sb("decay", [P, ST, CT * CT + CT + 2])
        turns = sb("turns", [P, 3, CS])
        phase = sb("phase", [P, CS + 1])
        phase_c = sb("phase_c", [P, CS])
        phase_b = sb("phase_b", [P, CS])
        hmv = sb("hmv", [P, 2, TT, 2])
        hstats = sb("hstats", [P, 2, TT, 6])
        hsm = sb("hsm", [P, 2, 3, TT])
        zn = t0.rearrange("p (t d) -> p t d", t=ST)
        mo = t0.rearrange("p (q n) -> p q n", q=2)
        hb = t1.rearrange("p (q t d) -> p q t d", q=2, t=TT)
        hn = t2.rearrange("p (q t d) -> p q t d", q=2, t=TT)
        hnt = t3.rearrange("p (q n) -> p q n", q=2)
        sg = t4.rearrange("p (q n) -> p q n", q=2)
        hf = bf.rearrange("p a b -> p (a b)")[:, 0:2 * FC * BT].rearrange("p (q c n) -> p q c n", q=2, c=FC)

        carried = sem("carried")
        x_in = [sem(f"x_in{i}") for i in range(2)]
        w_in = [sem(f"w_in{i}") for i in range(3)]
        small_in = sem("small_in")
        out_stored = sem("out_stored")
        pool_const = sem("pool_const")
        dve_const = sem("dve_const")
        w_hi_ready = sem("w_hi_ready")
        w_lo_ready = sem("w_lo_ready")
        mv_ready = sem("mv_ready")
        xn_ready = sem("xn_ready")
        xt_ps_ready = sem("xt_ps_ready")
        xt_ready = sem("xt_ready")
        xt_lo_ready = sem("xt_lo_ready")
        logits_ps_ready = sem("logits_ps_ready")
        gap_ready = sem("gap_ready")
        tanh_ready = sem("tanh_ready")
        gates_ready = sem("gates_ready")
        gates_ps_ready = sem("gates_ps_ready")
        gates_t_ready = sem("gates_t_ready")
        a_ps_ready = sem("a_ps_ready")
        b_ps_ready = sem("b_ps_ready")
        g_ps_ready = sem("g_ps_ready")
        silu_done = sem("silu_done")
        gated_done = sem("gated_done")
        hid_done = sem("hid_done")
        hi_done = sem("hi_done")
        lo_done = sem("lo_done")
        down_done = sem("down_done")
        half_out_ready = sem("half_out_ready")
        out_ps_ready = sem("out_ps_ready")
        residual_done = sem("residual_done")
        dve_prep = sem("dve_prep")
        pool_prep = sem("pool_prep")

        wm_in = sem("wm_in")
        conv_in = sem("conv_in")
        mixer_const = sem("mixer_const")
        mixer_const_act = sem("mixer_const_act")
        mixer_const_dve = sem("mixer_const_dve")
        (amv_ready, arstd_ready, zn_ready, zt_ps_ready, zt_ready, proj_ps_ready, silu_u_done, silu_z_done, bct_ps_ready,
         bc_n2_ready, bc_norm_ready, bcn_ready, rep_ps_ready, softplus_parts, dt_ready, theta_ready, theta_max_ready,
         inv_ready, decay_args_ready, decays_ready, decay_big_ready, angle_in_ready, arctan_done, angle_ready,
         turns_ready, phase_c_ready, phase_b_ready, sine_c_done, sine_b_done, cf_ready, cfs_ready, bf_ready, cfx_ready,
         tm_ps_ready, tm_ready, gram_ps_ready, gram_ready, ds_ps_ready, state_ready, o_ps_ready, y_ready,
         mix_f_ps_ready, mix_f_ready, mix_ps_ready, hmv_ready, hr_ready, hn_ready, hnt_ps_ready, hnt_ready,
         gate_ps_ready, up_ps_ready, silu_g_done, hf_ready, ffn_ps_ready, ffn_f_ready, ffn_t_ps_ready, mixer_done,
         act_mix, dve_front, dve_tail, pool_mix) = (sem("m_" + n) for n in (
            "amv", "arstd", "zn", "zt_ps", "zt", "proj_ps", "silu_u", "silu_z", "bct_ps", "bc_n2", "bc_norm", "bcn",
            "rep_ps", "softplus", "dt", "theta", "theta_max", "inv", "decay_args", "decays", "decay_big", "angle_in",
            "arctan", "angle", "turns", "phase_c", "phase_b", "sine_c", "sine_b", "cf", "cfs", "bf", "cfx", "tm_ps",
            "tm", "gram_ps", "gram", "ds_ps", "state", "o_ps", "y", "mix_f_ps", "mix_f", "mix_ps", "hmv", "hr", "hn",
            "hnt_ps", "hnt", "gate_ps", "up_ps", "silu_g", "hf", "ffn_ps", "ffn_f", "ffn_t_ps", "mixer_done",
            "act_mix", "dve_front", "dve_tail", "pool_mix"))

        PREP_DVE = 16
        PREP_POOL = 2
        POOL_MIX = 12
        ACT_MIX = 4
        DVE_FRONT = 39
        DVE_TAIL = 9

        def apart(eng):
            eng.sem_inc(carried, 1)

        def tiles(blk):
            return bass.ds(blk * TT, TT)

        def half(turn, size=BT):
            if isinstance(turn, int):
                return bass.ds((turn % 2) * size, size)
            return bass.ds((turn & 1) * size, size)

        block = ctx.enter_context(nc.Block())

        @block.sync
        def _(sp):
            xv = A["L0_attn_x"].rearrange("b (t p) d -> p (b t) d", p=P)
            sp.dma_start(x[:, 0:TT, :], xv[:, 0:TT, :]).then_inc(x_in[0], 16)
            sp.dma_start(w_raw[:, 0, 0:HID], A["L0_ffn_sw1"]).then_inc(w_in[0], 16)
            sp.dma_start(w_raw[:, 0, HID:2 * HID], A["L0_ffn_sw2"]).then_inc(w_in[0], 16)
            sp.dma_start(w_raw[:, 0, 2 * HID:].rearrange("p (k d) -> p k d", k=2),
                         A["L0_ffn_sw3"].rearrange("(k p) d -> p k d", p=P)).then_inc(w_in[0], 16)
            sp.dma_start(rw[:, :], A["L0_ffn_rw"]).then_inc(small_in, 16)
            for t in range(TT):
                sp.dma_start(rb[:, t, :], A["L0_ffn_rb"].rearrange("(a e) -> a e", a=1).broadcast_to([P, NE])).then_inc(small_in, 16)
            for n in range(2):
                es = slice(4 * n, 4 * n + 4)
                ws = slice(1 + 4 * n, 5 + 4 * n)
                sp.dma_start(w_raw[:, ws, 0:HID],
                             A["L0_ffn_ew1"][es].rearrange("e d h -> d e h")).then_inc(w_in[1 + n], 16)
                sp.dma_start(w_raw[:, ws, HID:2 * HID],
                             A["L0_ffn_ew2"][es].rearrange("e d h -> d e h")).then_inc(w_in[1 + n], 16)
                for e in range(4 * n, 4 * n + 4):
                    sp.dma_start(w_raw[:, 1 + e, 2 * HID:].rearrange("p (k d) -> p k d", k=2),
                                 A["L0_ffn_ew3"][e].rearrange("(k p) d -> p k d", p=P)).then_inc(w_in[1 + n], 16)
            sp.dma_start(x[:, TT:, :], xv[:, TT:, :]).then_inc(x_in[1], 16)
            sp.dma_start(col[:, :], A["columns"]).then_inc(conv_in, 16)
            sp.wait_ge(residual_done, NB)
            sp.dma_start(bf.rearrange("p a b -> p (a b)")[:, 0:TAPS * (DI + 2 * DS)],
                         A["conv_taps"].broadcast_to([P, TAPS * (DI + 2 * DS)])).then_inc(conv_in, 16)
            sp.dma_start(t0[:, 0:548], A["in_proj_t"]).then_inc(conv_in, 16)
            sp.dma_start(w_z[:, :], A["in_proj_t"][:, 0:DI]).then_inc(wm_in, 16)
            sp.dma_start(w_out[:, :, :], A["out_proj_t"].rearrange("(k p) d -> p k d", p=P)).then_inc(wm_in, 16)
            sp.dma_start(w_gate[:, :], A["gate_t"]).then_inc(wm_in, 16)
            sp.dma_start(w_up[:, :], A["up_t"]).then_inc(wm_in, 16)
            sp.dma_start(w_down[:, 0:2, :], A["down_t"][0:2 * P].rearrange("(k p) d -> p k d", p=P)).then_inc(wm_in, 16)
            sp.dma_start(w_down[0:FF - 2 * P, 2, :], A["down_t"][2 * P:FF]).then_inc(wm_in, 16)
            ov = out.rearrange("b (t p) d -> p (b t) d", p=P)
            for n in range(NB):
                sp.wait_ge(residual_done, NB + n + 1)
                sp.dma_start(ov[:, n * TT:(n + 1) * TT, :], x[:, n * TT:(n + 1) * TT, :]).then_inc(out_stored, 16)
            sp.wait_ge(out_stored, 16 * NB)

        W_LOADS = [48] + [96] * 2

        def weights_loaded(eng, e):
            n = 0 if e == 0 else 1 + (e - 1) // 4
            eng.wait_ge(w_in[n], W_LOADS[n])

        def pool_rstd(pool, turn):
            own = Steps(pool, pool_prep, PREP_POOL, turn)
            pool.wait_ge(mv_ready, turn + 1)
            apart(pool)
            own.step(pool.tensor_scalar(var_eps[:, :], mv[:, :, 1], LN_EPS, None, ALU.add))
            own.settle()
            own.step(pool.tensor_tensor(rstd[:, :], var_eps[:, :], minus_half[:, :], ALU.pow))
            own.close()

        def pool_xt_lo(pool, turn):
            pool.wait_ge(xt_ready, 2 * turn + 2)
            pool.tensor_tensor(xt_lo[:, half(turn)], xt[:, :], xt_hi[:, half(turn)].bitcast(F32),
                               ALU.subtract).then_inc(xt_lo_ready, 1)

        def pool_step(pool, turn, s):
            n = turn * STEPS + s
            pool.wait_ge(hi_done, n + 1)
            if not (isinstance(turn, int) and n < 3):
                pool.wait_ge(down_done, n - 2)
            pool.tensor_tensor(hid_lo[:, s % 3, :], hid[:, s % 2, :], hid_hi[:, s % 3, :].bitcast(F32),
                               ALU.subtract).then_inc(lo_done, 1)

        def pool_block(pool, call, blk, last=False):
            turn = blk + call * NB
            for s in range(STEPS):
                pool_step(pool, turn, s)
                if s == 4 and not last:
                    pool_rstd(pool, turn + 1)
                if s == 8 and not last:
                    pool_xt_lo(pool, turn + 1)

        def pool_ffn(pool, call):
            pool_rstd(pool, call * NB)
            pool_xt_lo(pool, call * NB)
            pool_block(pool, call, 0)
            with pool.Fori(1, NB - 1) as blk:
                pool_block(pool, call, blk)
            pool_block(pool, call, NB - 1, last=True)

        def pool_mixer_const(pool):
            pool.wait_ge(residual_done, NB)
            m = mixer_const
            pool.memset(restart[:, :, :], 1.0).then_inc(m, 1)
            pool.memset(restart_small[:, :, :], 1.0).then_inc(m, 1)
            pool.memset(causal[:, :, :, :], 1.0).then_inc(m, 1)
            pool.memset(own_head[:, :], 1.0).then_inc(m, 1)
            pool.memset(cfx, 0.0).then_inc(m, 1)
            pool.memset(gram[:, :, :, :, :], 0.0).then_inc(m, 1)
            pool.memset(zt[:, 0:TAPS - 1], 0.0).then_inc(m, 1)
            pool.memset(minus_half8[:, :], -0.5).then_inc(m, 1)
            pool.memset(half16[:, :], 0.5).then_inc(m, 1)
            pool.memset(phase[:, 0:1], 0.0).then_inc(m, 1)
            pool.memset(pow_in[:, 0:1], float(np.e)).then_inc(m, 1)
            pool.wait_ge(conv_in, 48)
            pool.tensor_scalar(pow_in[:, 1:2], col[:, C_ALOG:C_ALOG + 1], 0.5, None, ALU.mult).then_inc(m, 1)
            pool.tensor_scalar(pow_in[:, 2:3], col[:, C_ALOG:C_ALOG + 1], -0.5, None, ALU.mult).then_inc(m, 1)
            pool.wait_ge(m, 13)
            pool.memset(restart[:, :, 0:1], 0.0).then_inc(m, 1)
            pool.memset(restart_small[:, :, 0:1], 0.0).then_inc(m, 1)
            pool.affine_select(out=causal[:, :, :, :], in_=causal[:, :, :, :], compare_op=ALU.is_ge, fill=0.0, base=0,
                               pattern=[[CH, CT], [0, NH], [1, CH]], channel_multiplier=-1).then_inc(m, 1)
            pool.affine_select(out=own_head[:, :], in_=own_head[:, :], compare_op=ALU.is_ge, fill=0.0, base=0,
                               pattern=[[-CH, NH], [0, DH]], channel_multiplier=1).then_inc(m, 1)
            pool.tensor_tensor(root_a[:, :], pow_in[:, 0:1], pow_in[:, 1:2], ALU.pow).then_inc(m, 1)
            pool.tensor_tensor(root_a_inv[:, :], pow_in[:, 0:1], pow_in[:, 2:3], ALU.pow).then_inc(m, 1)
            pool.wait_ge(m, 19)
            pool.affine_select(out=own_head[:, :], in_=own_head[:, :], compare_op=ALU.is_ge, fill=0.0, base=CH - 1,
                               pattern=[[CH, NH], [0, DH]], channel_multiplier=-1).then_inc(m, 1)
            pool.wait_ge(mixer_const_dve, 1)
            pool.memset(bf, 0.0).then_inc(m, 1)

        def pool_mixer(pool, b):
            own = Steps(pool, pool_mix, POOL_MIX, b)

            def step(instruction):
                own.step(instruction)
                own.settle()

            pool.wait_ge(amv_ready, b + 1)
            apart(pool)
            step(pool.tensor_scalar(asmall[:, 0, :], amv[:, :, 1], LN_EPS, None, ALU.add))
            step(pool.tensor_tensor(arstd[:, :], asmall[:, 0, :], minus_half8[:, :], ALU.pow))
            step(pool.tensor_tensor(asmall[:, 1, :], arstd[:, :], arstd[:, :], ALU.mult))
            step(pool.tensor_tensor(asmall[:, 2, :], asmall[:, 1, :], amv[:, :, 1], ALU.mult))
            apart(pool)
            step(pool.tensor_scalar(asmall[:, 3, :], asmall[:, 2, :], RMS_EPS, None, ALU.add))
            step(pool.tensor_tensor(asmall[:, 0, :], asmall[:, 3, :], minus_half8[:, :], ALU.pow))
            pool.tensor_tensor(azr[:, :], arstd[:, :], asmall[:, 0, :], ALU.mult).then_inc(arstd_ready, 1)
            pool.wait_ge(bc_n2_ready, b + 1)
            pool.tensor_tensor(bc_n[:, 1, :], bc_n[:, 0, :], half16[:, :], ALU.pow).then_inc(bc_norm_ready, 1)
            pool.wait_ge(cf_ready, b + 1)
            apart(pool)
            for h in range(NH):
                rows = slice(h * CH, (h + 1) * CH)
                pool.tensor_scalar(cfx[rows].rearrange("p t (j h c) -> p t j h c", j=CT, h=NH)[:, :, :, h, :],
                                   t4[rows].rearrange("p (t j c) -> p t j c", t=ST, j=CT),
                                   1.0, 0.0, ALU.mult, ALU.add).then_inc(cfx_ready, 1)
            for q in range(SQ):
                pool.wait_ge(hmv_ready, SQ * b + q + 1)
                step(pool.tensor_tensor(hsm[:, q, 0, :], hmv[:, q, :, 0], hmv[:, q, :, 0], ALU.mult))
                step(pool.tensor_tensor(hsm[:, q, 1, :], hsm[:, q, 0, :], hmv[:, q, :, 1], ALU.add))
                apart(pool)
                step(pool.tensor_scalar(hsm[:, q, 0, :], hsm[:, q, 1, :], RMS_EPS, None, ALU.add))
                pool.tensor_tensor(hsm[:, q, 2, :], hsm[:, q, 0, :], minus_half[:, :], ALU.pow).then_inc(hr_ready, 1)
            own.close()

        @block.gpsimd
        def _(pool):
            pool.memset(ident[:, :], 0.0).then_inc(pool_const, 1)
            pool.memset(minus_half[:, :], -0.5).then_inc(pool_const, 1)
            pool.memset(pick_f[:, :, :], 0.0).then_inc(pool_const, 1)
            pool.iota(iota[:, :, :], pattern=[[0, TT], [1, NE]], base=0, channel_multiplier=0,
                      allow_small_or_imprecise_dtypes=True).then_inc(pool_const, 1)
            pool.wait_ge(pool_const, 4)
            pool.affine_select(out=ident[:, :], in_=ident[:, :], compare_op=ALU.not_equal, fill=1.0, base=0,
                               pattern=[[-1, P]], channel_multiplier=1).then_inc(pool_const, 1)
            pool.affine_select(out=pick_f[:, :, :], in_=pick_f[:, :, :], compare_op=ALU.not_equal, fill=1.0, base=0,
                               pattern=[[-1, NE], [0, P]], channel_multiplier=1).then_inc(pool_const, 1)
            pool.wait_ge(pool_const, 6)
            pool.affine_select(out=pick_f[:, :, :], in_=pick_f[:, :, :], compare_op=ALU.not_equal, fill=1.0, base=-NE,
                               pattern=[[-1, NE], [0, P]], channel_multiplier=1).then_inc(pool_const, 1)
            pool_ffn(pool, 0)
            pool_mixer_const(pool)
            with pool.Fori(0, NSEQ) as b:
                pool_mixer(pool, b)
            pool_ffn(pool, 1)

        def act_w_hi(act, e):
            weights_loaded(act, e)
            act.activation(up_hi[:, e, :], w_raw[:, e, 0:2 * HID], ACT.Copy).then_inc(w_hi_ready, 1)
            act.activation(down_hi[:, e, :], w_raw[:, e, 2 * HID:], ACT.Copy).then_inc(w_hi_ready, 1)

        def act_xt(act, turn):
            act.wait_ge(xt_ps_ready, turn + 1)
            act.activation(xt[:, :], ps_t[:, :], ACT.Copy).then_inc(xt_ready, 1)
            act.activation(xt_hi[:, half(turn)], ps_t[:, :], ACT.Copy).then_inc(xt_ready, 1)

        def act_tanh(act, turn):
            act.wait_ge(gap_ready, turn + 1)
            act.activation(gap_tanh[:, :], gap[:, :], ACT.Tanh, scale=0.5).then_inc(tanh_ready, 1)

        def act_gates(act, turn):
            act.wait_ge(gates_ps_ready, turn + 1)
            act.activation(gates_t[:, half(turn)], ps_r[0:2 * NE, :], ACT.Copy).then_inc(gates_t_ready, 1)

        def act_half_out(act, turn):
            act.wait_ge(down_done, STEPS * (turn + 1))
            if not (isinstance(turn, int) and turn == 0):
                act.wait_ge(out_ps_ready, turn)
            act.activation(half_out[:, :], ps_o[:, :], ACT.Copy, scale=0.5).then_inc(half_out_ready, 1)

        def act_silu(act, turn, s):
            n = turn * STEPS + s
            act.wait_ge(a_ps_ready, n + 1)
            if not (isinstance(turn, int) and n < 2):
                act.wait_ge(gated_done, n - 1)
            act.activation(silu_a[:, s % 2, :], ps_a[:, s % 2, :], ACT.Silu).then_inc(silu_done, 1)

        def act_hi(act, turn, s):
            n = turn * STEPS + s
            act.wait_ge(hid_done, n + 1)
            if not (isinstance(turn, int) and n < 3):
                act.wait_ge(down_done, n - 2)
            act.activation(hid_hi[:, s % 3, :], hid[:, s % 2, :], ACT.Copy).then_inc(hi_done, 1)

        def act_block(act, call, blk, first=False, last=False):
            turn = blk + call * NB
            for s in range(STEPS):
                if s == LAG and not first:
                    act_half_out(act, turn - 1)
                act_silu(act, turn, s)
                if s >= 1:
                    act_hi(act, turn, s - 1)
                if call == 0 and first and s % 2 == 0 and s // 2 + 2 < NX:
                    act_w_hi(act, s // 2 + 2)
                if s == 7 and not last:
                    act_xt(act, turn + 1)
                if s == 12 and not last:
                    act_tanh(act, turn + 1)
                if s == 15 and not last:
                    act_gates(act, turn + 1)
            act_hi(act, turn, STEPS - 1)

        def act_ffn(act, call):
            act_xt(act, call * NB)
            act_tanh(act, call * NB)
            act_gates(act, call * NB)
            act_block(act, call, 0, first=True)
            with act.Fori(1, NB - 1) as blk:
                act_block(act, call, blk)
            act_block(act, call, NB - 1, last=True)
            act_half_out(act, call * NB + NB - 1)

        def act_mixer_const(act):
            act.wait_ge(conv_in, 48)
            act.activation(w_dt.rearrange("p (h c) -> p h c", h=NH),
                           t0[:, 2 * DI + 2 * DS:548].rearrange("p (h a) -> p h a", a=1).broadcast_to([P, NH, 2 * DS]),
                           ACT.Copy).then_inc(mixer_const_act, 1)
            act.wait_ge(mixer_const, 21)
            act.wait_ge(wm_in, 96)

        def act_mixer(act, b):
            own = Steps(act, act_mix, ACT_MIX, b)

            def step(instruction):
                own.step(instruction)
                own.settle()

            act.wait_ge(zt_ps_ready, b + 1)
            act.activation(zt[:, TAPS - 1:].rearrange("p (q n) -> p q n", q=2), ps_tr[:, :, :], ACT.Copy,
                           scale=col[:, C_NORM1:C_NORM1 + 1]).then_inc(zt_ready, 1)
            for k, source in enumerate((ps_a, ps_b)):
                act.wait_ge(proj_ps_ready, 6 * b + k + 1)
                act.activation(us[:, k, :], source[:, :, :].rearrange("p q n -> p (q n)"), ACT.Silu,
                               bias=col[:, C_CONVB + k:C_CONVB + k + 1]).then_inc(silu_u_done, 1)
            act.wait_ge(proj_ps_ready, 6 * b + 3)
            act.activation(bc_act, ps_go[0:2 * DS, :, :].rearrange("p q n -> p (q n)"), ACT.Silu,
                           bias=col[0:2 * DS, C_CONVBC:C_CONVBC + 1]).then_inc(silu_u_done, 1)
            for k, source in enumerate((ps_a, ps_b)):
                act.wait_ge(proj_ps_ready, 6 * b + 5 + k)
                act.activation(zs[:, k, :], source[:, :, :].rearrange("p q n -> p (q n)"), ACT.Silu).then_inc(silu_z_done, 1)
            dt_raw = ps_tr[:, :, :].rearrange("p q n -> p (q n)")
            act.activation(t1, dt_raw, ACT.Relu, bias=col[:, C_DTB:C_DTB + 1])
            step(act.activation(t0, dt_raw, ACT.Abs, bias=col[:, C_DTB:C_DTB + 1]))
            step(act.activation(t0, t0, ACT.Exp, scale=-1.0))
            act.activation(t0, t0, ACT.Ln, bias=1.0).then_inc(softplus_parts, 1)
            act.wait_ge(dt_ready, b + 1)
            step(act.activation(t0, t1, ACT.Square, scale=root_a[:, :]))
            act.activation(t2, t1, ACT.Copy, scale=root_a[:, :])
            act.activation(t3, t0, ACT.Ln, bias=1.0).then_inc(theta_ready, 1)
            act.wait_ge(theta_max_ready, b + 1)
            step(act.activation(t4, t4, ACT.Ln))
            act.activation(t4, t4, ACT.Exp, scale=-0.5).then_inc(inv_ready, 1)
            act.wait_ge(decay_args_ready, b + 1)
            act.activation(decay[:, :, :], decay[:, :, :], ACT.Exp, scale=-0.5).then_inc(decays_ready, 1)
            act.wait_ge(decay_big_ready, b + 1)
            act.activation(cfs, cfs, ACT.Exp, scale=-0.5).then_inc(decays_ready, 1)
            act.activation(t3, t3, ACT.Exp, scale=0.5).then_inc(decays_ready, 1)
            act.wait_ge(angle_in_ready, b + 1)
            act.activation(t2, t2, ACT.Arctan).then_inc(arctan_done, 1)
            act.wait_ge(angle_ready, b + 1)
            act.activation(t2, t2, ACT.Abs, scale=float(1 / (2 * np.pi))).then_inc(turns_ready, 1)
            act.wait_ge(phase_c_ready, b + 1)
            act.activation(t4, t4, ACT.Sin, scale=TWO_PI).then_inc(sine_c_done, 1)
            act.wait_ge(phase_b_ready, b + 1)
            act.activation(t0, t0, ACT.Sin, scale=TWO_PI).then_inc(sine_b_done, 1)
            for k in range(ST):
                act.wait_ge(tm_ps_ready, ST * b + k + 1)
                if k >= 2:
                    act.wait_ge(o_ps_ready, ST * b + k - 1)
                act.activation(tm[:, k % 2, :], ps_tr[:, k % 2, 0:DI + P], ACT.Copy).then_inc(tm_ready, 1)
            for q in range(SQ):
                act.wait_ge(mix_f_ps_ready, SQ * b + q + 1)
                act.activation(mo[:, q, :], ps_go[:, q, :], ACT.Copy).then_inc(mix_f_ready, 1)
            for q in range(SQ):
                act.wait_ge(hnt_ps_ready, SQ * b + q + 1)
                act.activation(hnt[:, q, :], ps_tr[:, q, :], ACT.Copy,
                               scale=col[:, C_NORM2:C_NORM2 + 1]).then_inc(hnt_ready, 1)
            for q in range(SQ):
                for c in range(FC):
                    n = q * FC + c
                    rows = slice(0, min(P, FF - c * P))
                    act.wait_ge(gate_ps_ready, SQ * FC * b + n + 1)
                    if n >= 2:
                        act.wait_ge(hf_ready, SQ * FC * b + n - 1)
                    act.activation(sg[rows, n % 2, :], ps_a[rows, n % 2, :], ACT.Silu).then_inc(silu_g_done, 1)
            for q in range(SQ):
                act.wait_ge(ffn_ps_ready, SQ * b + q + 1)
                act.activation(mo[:, q, :], ps_go[:, q, :], ACT.Copy).then_inc(ffn_f_ready, 1)
            own.close()

        @block.scalar
        def _(act):
            act.wait_ge(pool_const, 7)
            act.activation(pick[:, :, :], pick_f[:, :, :], ACT.Copy).then_inc(dve_const, 1)
            act_w_hi(act, 0)
            act_w_hi(act, 1)
            act_ffn(act, 0)
            act_mixer_const(act)
            with act.Fori(0, NSEQ) as b:
                act_mixer(act, b)
            act_ffn(act, 1)

        def dve_w_lo(dve, e):
            weights_loaded(dve, e)
            dve.wait_ge(w_hi_ready, 2 * e + 2)
            dve.tensor_tensor(up_lo[:, e, :], w_raw[:, e, 0:2 * HID], up_hi[:, e, :].bitcast(F32),
                              ALU.subtract).then_inc(w_lo_ready, 1)
            dve.tensor_tensor(down_lo[:, e, :], w_raw[:, e, 2 * HID:], down_hi[:, e, :].bitcast(F32),
                              ALU.subtract).then_inc(w_lo_ready, 1)

        def dve_stats(dve, own, call, blk):
            turn = blk + call * NB
            for t in range(TT):
                own.step(dve.bn_stats(stats[:, t, :], x[:, bass.ds(blk * TT + t, 1), :]))
            own.settle()
            apart(dve)
            for t in range(TT):
                r = dve.bn_aggr(mv[:, t, :], stats[:, t, :])
            r.then_inc(mv_ready, 1)

        def dve_norm(dve, call, blk):
            turn = blk + call * NB
            dve.wait_ge(mv_ready, turn + 1)
            dve.wait_ge(pool_prep, PREP_POOL * (turn + 1))
            if not (isinstance(turn, int) and turn == 0):
                dve.wait_ge(xt_ps_ready, turn)
            for t in range(TT):
                r = dve.tensor_scalar(xn[:, t, :], x[:, bass.ds(blk * TT + t, 1), :], mv[:, t, 0:1], rstd[:, t:t + 1],
                                      ALU.subtract, ALU.mult)
            r.then_inc(xn_ready, 1)

        def dve_route(dve, own, turn):
            dve.wait_ge(logits_ps_ready, turn + 1)
            own.step(dve.tensor_tensor(logits[:, :, :], ps_r[:, 0:TT * NE].rearrange("p (t e) -> p t e", t=TT),
                                       rb[:, :, :], ALU.add))
            own.settle()
            apart(dve)
            for t in range(TT):
                r = dve.max(top[:, t, :], logits[:, t, :])
            own.step(r)
            own.settle()
            dve.tensor_tensor(gap[:, :], top[:, :, 0], top[:, :, 1], ALU.subtract).then_inc(gap_ready, 1)
            for t in range(TT):
                r = dve.max_index(top_i[:, t, :], top[:, t, :], logits[:, t, :])
            own.step(r)
            own.settle()
            own.step(dve.tensor_copy(top_f[:, :, :], top_i[:, :, 0:2]))
            own.settle()
            for k in range(2):
                own.step(dve.tensor_tensor(hot[:, k, :, :], iota[:, :, :],
                                           top_f[:, :, k:k + 1].broadcast_to([P, TT, NE]), ALU.is_equal))

        def dve_gates(dve, own, turn):
            dve.wait_ge(tanh_ready, turn + 1)
            own.step(dve.tensor_scalar(share[:, 0, :], gap_tanh[:, :], 0.5, 0.5, ALU.mult, ALU.add))
            own.step(dve.tensor_scalar(share[:, 1, :], gap_tanh[:, :], -0.5, 0.5, ALU.mult, ALU.add))
            own.settle()
            for k in range(2):
                own.step(dve.tensor_tensor(hot[:, k, :, :], hot[:, k, :, :],
                                           share[:, k, :].rearrange("p (t a) -> p t a", a=1).broadcast_to([P, TT, NE]),
                                           ALU.mult))
            own.settle()
            own.step(dve.tensor_tensor(gate[:, :, :], hot[:, 0, :, :], hot[:, 1, :, :], ALU.add))
            own.settle()
            if not (isinstance(turn, int) and turn == 0):
                dve.wait_ge(gates_ps_ready, turn)
            own.step(dve.tensor_copy(gate_parts[:, :, 0:NE].bitcast(F32R), gate[:, :, :]))
            own.settle()
            dve.tensor_tensor(gate_parts[:, :, NE:], gate[:, :, :], gate_parts[:, :, 0:NE],
                              ALU.subtract).then_inc(gates_ready, 1)

        def dve_residual(dve, call, blk):
            turn = blk + call * NB
            dve.wait_ge(out_ps_ready, turn + 1)
            dve.tensor_tensor(x[:, tiles(blk), :], x[:, tiles(blk), :],
                              ps_t[:, :].rearrange("p (t d) -> p t d", t=TT), ALU.add).then_inc(residual_done, 1)

        def dve_step(dve, turn, s):
            n = turn * STEPS + s
            dve.wait_ge(silu_done, n + 1)
            if s < 2:
                source, done = silu_a[:, s % 2, :], None
            else:
                if s % 2 == 0:
                    dve.wait_ge(g_ps_ready, turn * NE + s // 2)
                dve.tensor_tensor(gated[:, s % 2, :], silu_a[:, s % 2, :], ps_g[:, :], ALU.mult).then_inc(gated_done, 1)
                dve.wait_ge(gated_done, n + 1)
                source = gated[:, s % 2, :]
            dve.wait_ge(b_ps_ready, n + 1)
            if not (isinstance(turn, int) and n < 2):
                dve.wait_ge(hi_done, n - 1)
                dve.wait_ge(lo_done, n - 1)
            r = dve.tensor_tensor(hid[:, s % 2, :], source, ps_b[:, s % 2, :], ALU.mult)
            r.then_inc(hid_done, 1)
            if s < 2:
                dve.wait_ge(hid_done, n + 1)
                dve.sem_inc(gated_done, 1)

        def dve_block(dve, call, blk, first=False, last=False):
            turn = blk + call * NB
            own = Steps(dve, dve_prep, PREP_DVE, turn + 1)
            for s in range(STEPS):
                dve_step(dve, turn, s)
                if call == 0 and first and s % 2 == 0 and s // 2 + 2 < NX:
                    dve_w_lo(dve, s // 2 + 2)
                if s == 3 and not last:
                    dve_stats(dve, own, call, blk + 1)
                if s == 4 and not first:
                    dve_residual(dve, call, blk - 1)
                if s == 5 and not last:
                    dve_norm(dve, call, blk + 1)
                if s == 11 and not last:
                    dve_route(dve, own, turn + 1)
                if s == 13 and not last:
                    dve_gates(dve, own, turn + 1)
            if not last:
                own.close()

        def dve_ffn(dve, call):
            own = Steps(dve, dve_prep, PREP_DVE, call * NB)
            dve_stats(dve, own, call, 0)
            dve_norm(dve, call, 0)
            if call == 0:
                dve_w_lo(dve, 0)
                dve_w_lo(dve, 1)
                dve.wait_ge(small_in, 16 * (1 + TT))
                dve.wait_ge(x_in[1], 16)
            dve_route(dve, own, call * NB)
            dve_gates(dve, own, call * NB)
            own.close()
            dve_block(dve, call, 0, first=True)
            with dve.Fori(1, NB - 1) as blk:
                dve_block(dve, call, blk)
            dve_block(dve, call, NB - 1, last=True)
            dve_residual(dve, call, NB - 1)

        def dve_mixer_const(dve):
            dve.wait_ge(residual_done, NB)
            dve.wait_ge(conv_in, 48)
            dve.wait_ge(mixer_const, 20)
            taps = bf.rearrange("p a b -> p (a b)")[:, 0:TAPS * (DI + 2 * DS)].rearrange("p (k c) -> p k c", k=TAPS)
            for k in range(TAPS):
                r = dve.tensor_tensor(w_tap[:, k, :], taps[:, k, :], t0[:, DI:2 * DI + 2 * DS], ALU.mult)
            r.then_inc(mixer_const_dve, 1)
            dve.wait_ge(mixer_const_act, 1)
            dve.wait_ge(mixer_const_dve, 1)
            dve.wait_ge(mixer_const, 21)

        def dve_mixer(dve, b):
            own = Steps(dve, dve_front, DVE_FRONT, b)

            def step(instruction):
                own.step(instruction)
                own.settle()

            def chunks(t):
                return t.rearrange("p (c n) -> p c n", c=CS)

            def spread(small):
                return small.rearrange("p (c a) -> p c a", a=1).broadcast_to([P, CS, CH])

            for t in range(ST):
                r = dve.bn_stats(astats[:, t, :], x[:, bass.ds(b * ST + t, 1), :])
            step(r)
            apart(dve)
            for t in range(ST):
                r = dve.bn_aggr(amv[:, t, :], astats[:, t, :])
            r.then_inc(amv_ready, 1)
            dve.wait_ge(amv_ready, b + 1)
            dve.wait_ge(arstd_ready, b + 1)
            for t in range(ST):
                r = dve.tensor_scalar(zn[:, t, :], x[:, bass.ds(b * ST + t, 1), :], amv[:, t, 0:1], azr[:, t:t + 1],
                                      ALU.subtract, ALU.mult)
            r.then_inc(zn_ready, 1)
            dve.wait_ge(bct_ps_ready, b + 1)
            step(dve.tensor_copy(bc_tm[:, :, :], ps_go[:, 0, 0:2 * ST * DS].rearrange("p (g n) -> p g n", n=DS)))
            step(dve.tensor_tensor(bc_sq[:, :, :], bc_tm[:, :, :], bc_tm[:, :, :], ALU.mult))
            dve.reduce_sum(bc_n[:, 0, :], bc_sq[:, :, :], axis=mybir.AxisListType.X).then_inc(bc_n2_ready, 1)
            dve.wait_ge(bc_norm_ready, b + 1)
            step(dve.tensor_scalar(bc_n[:, 2, :], bc_n[:, 1, :], RMS_EPS, None, ALU.add))
            step(dve.reciprocal(bc_n[:, 0, :], bc_n[:, 2, :]))
            dve.tensor_tensor(bc_rep,
                              bc_tm[:, :, :].rearrange("p g (a n) -> p g a n", a=1).broadcast_to([P, 2 * ST, 2 * NH, DS]),
                              bc_n[:, 0, :].rearrange("p (g a b) -> p g a b", a=1, b=1).broadcast_to([P, 2 * ST, 2 * NH, DS]),
                              ALU.mult).then_inc(bcn_ready, 1)
            dve.wait_ge(softplus_parts, b + 1)
            dve.tensor_tensor(t1, t0, t1, ALU.add).then_inc(dt_ready, 1)
            dve.wait_ge(theta_ready, b + 1)
            dve.wait_ge(rep_ps_ready, b + 1)
            dve.tensor_scalar(t4, t0, 1.0, None, ALU.max).then_inc(theta_max_ready, 1)
            dve.tensor_scalar(t0, t0, 1.0, float(-np.pi / 2), ALU.is_gt, ALU.mult)
            step(dve.tensor_tensor_scan(t5, restart[:, :, :].rearrange("p c n -> p (c n)"), t3, 0.0, ALU.mult, ALU.add))
            dve.tensor_copy(ctot[:, :, :].rearrange("p t j -> p (t j)"), chunks(t5)[:, :, CH - 1])
            step(dve.tensor_copy(cmid[:, :, :].rearrange("p t j -> p (t j)"), chunks(t5)[:, :, CH // 2 - 1]))
            step(dve.tensor_tensor_scan(cinc[:, :, :].rearrange("p t j -> p (t j)"),
                                        restart_small[:, :, :].rearrange("p t j -> p (t j)"),
                                        ctot[:, :, :].rearrange("p t j -> p (t j)"), 0.0, ALU.mult, ALU.add))
            step(dve.tensor_tensor(refs[:, :, :], cinc[:, :, :], ctot[:, :, :], ALU.subtract))
            step(dve.tensor_tensor(refs[:, :, :], refs[:, :, :], cmid[:, :, :], ALU.add))
            for j in range(CT):
                r = dve.tensor_tensor(decay[:, :, j * CT:(j + 1) * CT],
                                      refs[:, :, j:j + 1].broadcast_to([P, ST, CT]), refs[:, :, :], ALU.subtract)
            dve.tensor_copy(decay[:, :, CT * CT:CT * CT + CT], refs[:, :, :])
            dve.tensor_copy(decay[:, :, CT * CT + CT:CT * CT + CT + 1], cinc[:, :, CT - 1:CT])
            step(dve.tensor_tensor(decay[:, :, CT * CT + CT + 1:], cinc[:, :, CT - 1:CT], refs[:, :, CT - 1:CT],
                                   ALU.subtract))
            dve.tensor_scalar(decay[:, :, 0:CT * CT], decay[:, :, 0:CT * CT], 0.0, None,
                              ALU.max).then_inc(decay_args_ready, 1)
            mid = cmid[:, :, :].rearrange("p t j -> p (t j)")
            step(dve.tensor_tensor(chunks(t5), chunks(t5), spread(mid), ALU.subtract))
            step(dve.tensor_tensor(t3, t5, t3, ALU.subtract))
            dve.wait_ge(proj_ps_ready, 6 * b + 6)
            dve.tensor_scalar(cfs, t5, -CLAMP, None, ALU.max)
            dve.tensor_scalar(t3, t3, CLAMP, None, ALU.min).then_inc(decay_big_ready, 1)
            dve.wait_ge(inv_ready, b + 1)
            dve.tensor_tensor(t2, t2, t4, ALU.min).then_inc(angle_in_ready, 1)
            dve.wait_ge(arctan_done, b + 1)
            dve.tensor_tensor(t2, t2, t0, ALU.add).then_inc(angle_ready, 1)
            dve.wait_ge(turns_ready, b + 1)
            step(dve.tensor_tensor_scan(t0, restart[:, :, :].rearrange("p c n -> p (c n)"), t2, 0.0, ALU.mult, ALU.add))
            step(dve.tensor_copy(turns[:, 0, :], chunks(t0)[:, :, CH - 1]))
            step(dve.tensor_scalar(turns[:, 1, :], turns[:, 0, :], ROUND, -ROUND, ALU.add, ALU.add))
            step(dve.tensor_tensor(turns[:, 2, :], turns[:, 0, :], turns[:, 1, :], ALU.subtract))
            step(dve.tensor_tensor_scan(phase[:, 1:], turns[:, 2, :], turns[:, 2, :], 0.0, ALU.add, ALU.bypass))
            dve.tensor_scalar(phase_c[:, :], phase[:, 0:CS], col[:, C_OFFC:C_OFFC + 1], None, ALU.add)
            step(dve.tensor_scalar(phase_b[:, :], phase[:, 0:CS], col[:, C_OFFB:C_OFFB + 1], None, ALU.add))
            step(dve.tensor_tensor(chunks(t4), chunks(t0), spread(phase_c[:, :]), ALU.add))
            step(dve.tensor_scalar(t5, t4, ROUND, -ROUND, ALU.add, ALU.add))
            dve.tensor_tensor(t4, t4, t5, ALU.subtract).then_inc(phase_c_ready, 1)
            step(dve.tensor_tensor(t0, t0, t2, ALU.subtract))
            step(dve.tensor_tensor(chunks(t0), chunks(t0), spread(phase_b[:, :]), ALU.add))
            step(dve.tensor_scalar(t5, t0, ROUND, -ROUND, ALU.add, ALU.add))
            dve.tensor_tensor(t0, t0, t5, ALU.subtract).then_inc(phase_b_ready, 1)
            dve.wait_ge(rep_ps_ready, b + 1)
            dve.wait_ge(sine_c_done, b + 1)
            dve.wait_ge(decays_ready, 3 * b + 3)
            step(dve.scalar_tensor_tensor(t4, t4, root_a_inv[:, :], ps_b[:, :, :].rearrange("p q n -> p (q n)"),
                                          ALU.mult, ALU.mult))
            dve.tensor_tensor(t4, t4, cfs, ALU.mult).then_inc(cf_ready, 1)
            dve.wait_ge(cf_ready, b + 1)
            to_chunk = decay[:, :, CT * CT:CT * CT + CT].rearrange("p t (j a) -> p t j a", a=1)
            dve.tensor_tensor(cfs.rearrange("p (t j c) -> p t j c", t=ST, j=CT),
                              t4.rearrange("p (t j c) -> p t j c", t=ST, j=CT),
                              to_chunk.broadcast_to([P, ST, CT, CH]), ALU.mult).then_inc(cfs_ready, 1)
            dve.wait_ge(sine_b_done, b + 1)
            step(dve.tensor_tensor(t0, t0, ps_a[:, :, :].rearrange("p q n -> p (q n)"), ALU.mult))
            step(dve.tensor_tensor(t0, t0, t1, ALU.mult))
            diagonal = bass.AP(bf.tensor, bf.offset, [bf.ap[0], [CT * P, ST], [P + CH, CT], [1, CH]])
            step(dve.tensor_tensor(diagonal, t0.rearrange("p (t j c) -> p t j c", t=ST, j=CT),
                                   t3.rearrange("p (t j c) -> p t j c", t=ST, j=CT), ALU.mult))
            for j in range(1, CT):
                between = decay[:, :, j * CT:j * CT + j].rearrange("p t (i a) -> p t i a", a=1)
                r = dve.tensor_tensor(bf[:, :, j * P:j * P + j * CH].rearrange("p t (i c) -> p t i c", i=j),
                                      diagonal[:, :, 0:j, :], between.broadcast_to([P, ST, j, CH]), ALU.mult)
            r.then_inc(bf_ready, 1)
            step(dve.memset(state[:, 0, :], 0.0))

            def gram_copy(k):
                dve.wait_ge(gram_ps_ready, ST * b + k + 1)
                if k >= 2:
                    dve.wait_ge(o_ps_ready, ST * b + k - 1)
                apart(dve)
                dve.copy_predicated(gram[:, k % 2].rearrange("p j h c -> p (j h c)"),
                                    causal[:, :, :, :].rearrange("p j h c -> p (j h c)").bitcast(I16),
                                    ps_a[:, k % 2, :]).then_inc(gram_ready, 1)

            def state_update(k):
                dve.wait_ge(ds_ps_ready, ST * b + k + 1)
                last = CT * CT + CT
                step(dve.scalar_tensor_tensor(state_new[:, :], ps_go[:, 0, 0:DI], decay[:, k, last + 1:last + 2],
                                              own_head[:, :], ALU.mult, ALU.mult))
                if k >= 1:
                    dve.wait_ge(o_ps_ready, ST * b + k)
                dve.scalar_tensor_tensor(state[:, (k + 1) % 2, :], state[:, k % 2, :], decay[:, k, last:last + 1],
                                         state_new[:, :], ALU.mult, ALU.add).then_inc(state_ready, 1)

            def gated_output(q):
                dve.wait_ge(o_ps_ready, ST * b + TT * (q + 1))
                at = slice(q * BT, (q + 1) * BT)
                for k in range(2):
                    r = dve.scalar_tensor_tensor(us[:, k, at], us[:, k, at], col[:, C_D + k:C_D + k + 1], ps_b[:, k, :],
                                                 ALU.mult, ALU.add)
                step(r)
                dve.tensor_tensor(zs[:, :, at], zs[:, :, at], us[:, :, at], ALU.mult).then_inc(y_ready, 1)

            gram_copy(0)
            for k in range(ST):
                if k >= 1:
                    dve.wait_ge(state_ready, ST * b + k)
                state_update(k)
                if k + 1 < ST:
                    gram_copy(k + 1)
                if k % TT == TT - 1:
                    gated_output(k // TT)
            own.close()
            own = Steps(dve, dve_tail, DVE_TAIL, b)
            for q in range(SQ):
                for t in range(TT):
                    r = dve.tensor_scalar(hb[:, q, t, :], x[:, bass.ds(b * ST + q * TT + t, 1), :],
                                          amv[:, q * TT + t, 0:1], arstd[:, q * TT + t:q * TT + t + 1],
                                          ALU.subtract, ALU.mult)
                own.step(r)
            for q in range(SQ):
                xq = x[:, bass.ds(b * ST + q * TT, TT), :]
                dve.wait_ge(mix_ps_ready, SQ * b + q + 1)
                own.settle()
                own.step(dve.tensor_tensor(hb[:, q, :, :], hb[:, q, :, :],
                                           ps_tr[:, q, :].rearrange("p (t d) -> p t d", t=TT), ALU.add))
                own.settle()
                own.step(dve.tensor_tensor(xq, xq, hb[:, q, :, :], ALU.add))
                for t in range(TT):
                    r = dve.bn_stats(hstats[:, q, t, :], hb[:, q, t, :])
                own.step(r)
                own.settle()
                apart(dve)
                for t in range(TT):
                    r = dve.bn_aggr(hmv[:, q, t, :], hstats[:, q, t, :])
                r.then_inc(hmv_ready, 1)
            for q in range(SQ):
                dve.wait_ge(hr_ready, SQ * b + q + 1)
                for t in range(TT):
                    r = dve.tensor_scalar(hn[:, q, t, :], hb[:, q, t, :], hsm[:, q, 2, t:t + 1], None, ALU.mult)
                r.then_inc(hn_ready, 1)
            for q in range(SQ):
                for c in range(FC):
                    n = q * FC + c
                    rows = slice(0, min(P, FF - c * P))
                    dve.wait_ge(up_ps_ready, SQ * FC * b + n + 1)
                    dve.wait_ge(silu_g_done, SQ * FC * b + n + 1)
                    dve.tensor_tensor(hf[rows, q, c, :], sg[rows, n % 2, :], ps_b[rows, n % 2, :],
                                      ALU.mult).then_inc(hf_ready, 1)
            for q in range(SQ):
                xq = x[:, bass.ds(b * ST + q * TT, TT), :]
                dve.wait_ge(ffn_t_ps_ready, SQ * b + q + 1)
                dve.tensor_tensor(xq, xq, ps_tr[:, q, :].rearrange("p (t d) -> p t d", t=TT),
                                  ALU.add).then_inc(mixer_done, 1)
            dve.wait_ge(ffn_ps_ready, SQ * b + SQ)
            own.step(dve.memset(bf.rearrange("p a b -> p (a b)")[:, 0:SQ * FC * BT], 0.0))
            own.settle()
            own.close()

        @block.vector
        def _(dve):
            dve.wait_ge(pool_const, 7)
            dve.wait_ge(x_in[0], 16)
            dve_ffn(dve, 0)
            dve_mixer_const(dve)
            with dve.Fori(0, NSEQ) as b:
                dve_mixer(dve, b)
            dve.wait_ge(mixer_done, SQ * NSEQ)
            dve_ffn(dve, 1)

        def pe_xt(pe, turn):
            pe.wait_ge(xn_ready, turn + 1)
            if not (isinstance(turn, int) and turn < 1):
                pe.wait_ge(xt_ready, 2 * turn)
            if isinstance(turn, int) and turn % NB == 0:
                if turn > 0:
                    pe.wait_ge(residual_done, turn)
            elif not (isinstance(turn, int) and turn < 2):
                pe.wait_ge(residual_done, turn - 1)
            for t in range(TT):
                r = pe.transpose(ps_t[:, t * P:(t + 1) * P], xn[:, t, :], ident[:, :])
            r.then_inc(xt_ps_ready, 1)

        def pe_logits(pe, turn):
            pe.wait_ge(xt_ready, 2 * turn + 1)
            if not (isinstance(turn, int) and turn < 1):
                pe.wait_ge(gates_t_ready, turn)
            for t in range(TT):
                r = pe.matmul(ps_r[:, t * NE:(t + 1) * NE], xt[:, t * P:(t + 1) * P], rw[:, :], start=True, stop=True)
            r.then_inc(logits_ps_ready, 1)

        def pe_gates(pe, turn):
            pe.wait_ge(gates_ready, turn + 1)
            apart(pe)
            for t in range(TT):
                r = pe.transpose(ps_r[0:2 * NE, t * P:(t + 1) * P], gate_parts[:, t, :], ident[:, :])
            r.then_inc(gates_ps_ready, 1)

        def pe_out(pe, turn):
            pe.wait_ge(half_out_ready, turn + 1)
            if not (isinstance(turn, int) and turn >= 0 and (turn + 1) % NB == 0):
                pe.wait_ge(xt_ready, 2 * turn + 4)
            for t in range(TT):
                r = pe.transpose(ps_t[:, t * P:(t + 1) * P], half_out[:, t * P:(t + 1) * P], ident[:, :])
            r.then_inc(out_ps_ready, 1)

        def pe_up(pe, turn, s):
            n = turn * STEPS + s
            e, k = s // 2, s % 2
            if not (isinstance(turn, int) and n < 2):
                pe.wait_ge(silu_done, n - 1)
                pe.wait_ge(hid_done, n - 1)
            for target, ready, at in ((ps_a, a_ps_ready, k * P), (ps_b, b_ps_ready, HID + k * P)):
                pe.matmul(target[:, s % 2, :], up_hi[:, e, at:at + P], xt_hi[:, half(turn)], start=True, stop=False)
                pe.matmul(target[:, s % 2, :], up_hi[:, e, at:at + P], xt_lo[:, half(turn)], start=False, stop=False)
                pe.matmul(target[:, s % 2, :], up_lo[:, e, at:at + P], xt_hi[:, half(turn)], start=False,
                          stop=True).then_inc(ready, 1)
            if s >= 2 and k == 0:
                pe.wait_ge(gated_done, n)
                apart(pe)
                pe.matmul(ps_g[:, :], pick[:, e - 1, :], gates_t[:, half(turn)], start=True,
                          stop=True).then_inc(g_ps_ready, 1)

        def pe_down(pe, turn, s):
            n = turn * STEPS + s
            e, at = s // 2, (s % 2) * P
            pe.wait_ge(lo_done, n + 1)
            if s == 0 and not (isinstance(turn, int) and turn == 0):
                pe.wait_ge(half_out_ready, turn)
            pe.matmul(ps_o[:, :], down_hi[:, e, at:at + P], hid_hi[:, s % 3, :], start=(s == 0), stop=False)
            pe.matmul(ps_o[:, :], down_hi[:, e, at:at + P], hid_lo[:, s % 3, :], start=False, stop=False)
            r = pe.matmul(ps_o[:, :], down_lo[:, e, at:at + P], hid_hi[:, s % 3, :], start=False, stop=(s == STEPS - 1))
            r.then_inc(down_done, 1)

        def pe_block(pe, call, blk, first=False, last=False):
            turn = blk + call * NB
            pe.wait_ge(xt_lo_ready, turn + 1)
            pe.wait_ge(gates_t_ready, turn + 1)
            for s in range(STEPS):
                if call == 0 and first and s % 2 == 0:
                    pe.wait_ge(w_lo_ready, s + 2)
                pe_up(pe, turn, s)
                if s >= LAG:
                    pe_down(pe, turn, s - LAG)
                elif not first:
                    pe_down(pe, turn - 1, s - LAG + STEPS)
                if s == 3 and not first:
                    pe_out(pe, turn - 1)
                if s == 6 and not last:
                    pe_xt(pe, turn + 1)
                if s == 9 and not last:
                    pe_logits(pe, turn + 1)
                if s == 14 and not last:
                    pe_gates(pe, turn + 1)

        def pe_ffn(pe, call):
            pe_xt(pe, call * NB)
            pe_logits(pe, call * NB)
            pe_gates(pe, call * NB)
            pe_block(pe, call, 0, first=True)
            with pe.Fori(1, NB - 1) as blk:
                pe_block(pe, call, blk)
            pe_block(pe, call, NB - 1, last=True)
            end = call * NB + NB - 1
            for s in range(STEPS - LAG, STEPS):
                pe_down(pe, end, s)
            pe_out(pe, end)

        def pe_mixer_const(pe):
            pe.wait_ge(mixer_const, 21)
            pe.wait_ge(mixer_const_dve, 1)
            pe.wait_ge(mixer_const_act, 1)
            pe.wait_ge(wm_in, 96)

        def pe_mixer(pe, b):
            pe.wait_ge(zn_ready, b + 1)
            for t in range(ST):
                r = pe.transpose(ps_tr[:, t // TT, (t % TT) * P:(t % TT + 1) * P], zn[:, t, :], ident[:, :])
            r.then_inc(zt_ps_ready, 1)
            pe.wait_ge(zt_ready, b + 1)

            def project(target, weights, taps):
                for q in range(SQ):
                    for k in range(taps):
                        shift = q * BT + (k if taps > 1 else TAPS - 1)
                        r = pe.matmul(target[:, q, :], weights(k), zt[:, shift:shift + BT], start=(k == 0),
                                      stop=(k == taps - 1))
                r.then_inc(proj_ps_ready, 1)

            project(ps_a, lambda k: w_tap[:, k, 0:P], TAPS)
            project(ps_b, lambda k: w_tap[:, k, P:2 * P], TAPS)
            project(ps_go[0:2 * DS], lambda k: w_tap[:, k, DI:], TAPS)
            project(ps_tr, lambda k: w_dt, 1)
            pe.wait_ge(silu_u_done, 3 * b + 1)
            project(ps_a, lambda k: w_z[:, 0:P], 1)
            pe.wait_ge(silu_u_done, 3 * b + 2)
            project(ps_b, lambda k: w_z[:, P:], 1)
            pe.wait_ge(silu_u_done, 3 * b + 3)
            apart(pe)
            for t in range(ST):
                r = pe.transpose(ps_go[:, 0, t * 2 * DS:(t + 1) * 2 * DS], bc_act[:, t * P:(t + 1) * P],
                                 ident[0:2 * DS, 0:2 * DS])
            r.then_inc(bct_ps_ready, 1)
            pe.wait_ge(bcn_ready, b + 1)
            pe.wait_ge(silu_z_done, 2 * b + 2)
            for n, target in ((0, ps_a), (1, ps_b)):
                for t in range(ST):
                    rep = bc_rep[:, 2 * t + n].rearrange("p r n -> p (r n)")
                    r = pe.transpose(target[:, t // TT, (t % TT) * P:(t % TT + 1) * P], rep, ident[:, :])
            r.then_inc(rep_ps_ready, 1)

            def token_major(k):
                if k >= 2:
                    pe.wait_ge(tm_ready, ST * b + k - 1)
                for p in range(2):
                    pe.transpose(ps_tr[:, k % 2, p * P:(p + 1) * P], us[:, p, k * P:(k + 1) * P], ident[:, :])
                pe.transpose(ps_tr[:, k % 2, DI:DI + P], bf[:, k, (CT - 1) * P:CT * P],
                             ident[:, :]).then_inc(tm_ps_ready, 1)

            def make_gram(k):
                if k >= 2:
                    pe.wait_ge(gram_ready, ST * b + k - 1)
                for j in range(CT):
                    r = pe.matmul(ps_a[:, k % 2, j * P:(j + 1) * P], bf[:, k, j * P:(j + 1) * P],
                                  cfx[:, k, j * P:(j + 1) * P], start=True, stop=True)
                r.then_inc(gram_ps_ready, 1)

            def outputs(k):
                pe.wait_ge(tm_ready, ST * b + k + 1)
                if k >= 1:
                    pe.wait_ge(state_ready, ST * b + k)
                pe.matmul(ps_go[:, 0, 0:DI], tm[:, k % 2, DI:], tm[:, k % 2, 0:DI], start=True,
                          stop=True).then_inc(ds_ps_ready, 1)
                pe.wait_ge(gram_ready, ST * b + k + 1)
                if k >= TT:
                    pe.wait_ge(y_ready, SQ * b + 1)
                at = slice((k % TT) * P, (k % TT + 1) * P)
                for p in range(2):
                    pe.matmul(ps_b[:, p, at], state[:, k % 2, p * P:(p + 1) * P], cfs[:, k * P:(k + 1) * P],
                              start=True, stop=False)
                    for i in range(2):
                        h = 2 * p + i
                        r = pe.matmul(ps_b[i * DH:(i + 1) * DH, p, at], tm[:, k % 2, h * DH:(h + 1) * DH],
                                      gram[:, k % 2, :, h, :], start=False, stop=True)
                r.then_inc(o_ps_ready, 1)

            pe.wait_ge(bf_ready, b + 1)
            pe.wait_ge(cfs_ready, b + 1)
            token_major(0)
            pe.wait_ge(cfx_ready, NH * b + NH)
            make_gram(0)
            for k in range(ST):
                if k + 1 < ST:
                    token_major(k + 1)
                    make_gram(k + 1)
                outputs(k)
            for q in range(SQ):
                pe.wait_ge(y_ready, SQ * b + q + 1)
                if q == 0:
                    pe.wait_ge(state_ready, ST * b + ST)
                for k in range(2):
                    r = pe.matmul(ps_go[:, q, :], w_out[:, k, :], zs[:, k, q * BT:(q + 1) * BT], start=(k == 0),
                                  stop=(k == 1))
                r.then_inc(mix_f_ps_ready, 1)

            def back(q):
                for t in range(TT):
                    r = pe.transpose(ps_tr[:, q, t * P:(t + 1) * P], mo[:, q, t * P:(t + 1) * P], ident[:, :])
                return r

            for q in range(SQ):
                pe.wait_ge(mix_f_ready, SQ * b + q + 1)
                if q == 0:
                    pe.wait_ge(tm_ready, ST * b + ST)
                back(q).then_inc(mix_ps_ready, 1)
            for q in range(SQ):
                pe.wait_ge(hn_ready, SQ * b + q + 1)
                for t in range(TT):
                    r = pe.transpose(ps_tr[:, q, t * P:(t + 1) * P], hn[:, q, t, :], ident[:, :])
                r.then_inc(hnt_ps_ready, 1)
            for q in range(SQ):
                pe.wait_ge(hnt_ready, SQ * b + q + 1)
                for c in range(FC):
                    n = q * FC + c
                    m = min(P, FF - c * P)
                    if n >= 2:
                        pe.wait_ge(hf_ready, SQ * FC * b + n - 1)
                    pe.matmul(ps_a[0:m, n % 2, :], w_gate[:, c * P:c * P + m], hnt[:, q, :], start=True,
                              stop=True).then_inc(gate_ps_ready, 1)
                    pe.matmul(ps_b[0:m, n % 2, :], w_up[:, c * P:c * P + m], hnt[:, q, :], start=True,
                              stop=True).then_inc(up_ps_ready, 1)
            for q in range(SQ):
                for c in range(FC):
                    m = min(P, FF - c * P)
                    pe.wait_ge(hf_ready, SQ * FC * b + q * FC + c + 1)
                    r = pe.matmul(ps_go[:, q, :], w_down[0:m, c, :], hf[0:m, q, c, :], start=(c == 0),
                                  stop=(c == FC - 1))
                r.then_inc(ffn_ps_ready, 1)
            for q in range(SQ):
                pe.wait_ge(ffn_f_ready, SQ * b + q + 1)
                back(q).then_inc(ffn_t_ps_ready, 1)
            pe.wait_ge(mixer_done, SQ * b + SQ)

        @block.tensor
        def _(pe):
            pe.wait_ge(pool_const, 7)
            pe.wait_ge(dve_const, 1)
            pe.wait_ge(small_in, 16 * (1 + TT))
            pe_ffn(pe, 0)
            pe_mixer_const(pe)
            with pe.Fori(0, NSEQ) as b:
                pe_mixer(pe, b)
            pe_ffn(pe, 1)


_OUT_SHAPE = (NSEQ, SEQ, P)


def kernel(**inputs):
    import concourse.bacc as bacc
    from concourse.bass_utils import run_bass_kernel_spmd as run

    arrays = laid_out(inputs)
    nc = bacc.Bacc("TRN2", target_bir_lowering=False, num_devices=1)
    A = {n: nc.dram_tensor("in_" + n, a.shape, mybir.dt.from_np(a.dtype), kind="ExternalInput").ap()
         for n, a in arrays.items()}
    out = nc.dram_tensor("out", _OUT_SHAPE, F32, kind="ExternalOutput").ap()
    macaron(nc, A, out)
    r = run(nc, [{"in_" + n: a for n, a in arrays.items()}], core_ids=[0])
    return r.results[0]["out"]


def laid_out(inputs):
    get = {n: np.ascontiguousarray(a) for n, a in inputs.items()}
    m = {n[8:]: a for n, a in get.items() if n.startswith("L0_attn_")}
    arrays = {n: a for n, a in get.items() if n.startswith("L0_ffn_")}
    arrays["L0_attn_x"] = m["x"]
    arrays["in_proj_t"] = np.ascontiguousarray(m["in_proj_w"].T)
    arrays["out_proj_t"] = np.ascontiguousarray(m["out_proj_w"].T)
    arrays["gate_t"] = np.ascontiguousarray(m["gate_w"].T)
    arrays["up_t"] = np.ascontiguousarray(m["up_w"].T)
    arrays["down_t"] = np.ascontiguousarray(m["down_w"].T)
    arrays["conv_taps"] = np.ascontiguousarray(m["conv_w"].T).reshape(1, TAPS * (DI + 2 * DS))
    col = np.zeros((P, NCOL), np.float32)
    col[:, C_NORM1] = m["norm1_w"]
    col[:, C_NORM2] = m["norm2_w"]
    col[:, C_CONVB:C_CONVB + 2] = m["conv_b"][0:DI].reshape(2, P).T
    col[0:2 * DS, C_CONVBC] = m["conv_b"][DI:]
    col[:, C_ALOG] = np.repeat(m["A_log"][:, None, :], 2, axis=1).reshape(P)
    col[:, C_DTB] = np.repeat(m["dt_bias"], 2 * DS)
    col[:, C_D:C_D + 2] = np.repeat(m["D"], DH).reshape(2, P).T
    part = (np.arange(P) // DS) % 2
    col[:, C_OFFC] = np.where(part == 0, 0.0, 0.25)
    col[:, C_OFFB] = np.where(part == 0, 0.25, 0.5)
    arrays["columns"] = col
    return arrays
```

```python
import numpy as np
import concourse.bass as bass
from concourse import mybir
from contextlib import ExitStack

F32 = mybir.dt.float32
F32R = mybir.dt.float32r
U32 = mybir.dt.uint32
I16 = mybir.dt.int16
BF16 = mybir.dt.bfloat16
ALU = mybir.AluOpType
ACT = mybir.ActivationFunctionType

P = 128
TOK = 4096
BT = 512
NB = TOK // BT
TT = BT // P
HID = 256
NE = 8
NX = NE + 1
STEPS = 2 * NX
LAG = 2
LN_EPS = 1e-5

NSEQ = 4
SEQ = TOK // NSEQ
SQ = SEQ // BT
DI = 256
NH = 4
DH = DI // NH
DS = 16
TAPS = 4
CH = 32
CT = P // CH
CB = BT // CH
FF = 352
FC = 3
RMS_EPS = 1e-6
IN_COLS = 2 * DI + 2 * DS + NH
ROUND = 1.5 * 2 ** 23
TWO_PI = 6.283185
CLAMP = 160.0
C_NORM1, C_NORM2, C_CONVB, C_CONVBC, C_ALOG, C_DTB, C_D, C_OFFC, C_OFFB = 0, 1, 2, 4, 5, 6, 7, 9, 10
NCOL = 11
ARENA = 22880


class Steps:

    def __init__(self, eng, sem, per, turn):
        self.eng, self.sem, self.per, self.turn, self.k = eng, sem, per, turn, 0

    def step(self, instruction):
        self.k += 1
        instruction.then_inc(self.sem, 1)

    def settle(self):
        self.eng.wait_ge(self.sem, self.turn * self.per + self.k)

    def close(self):
        assert self.k == self.per, (self.k, self.per)


def macaron(nc, A, out):
    ctx = ExitStack()
    with ctx:
        def sb(name, shape, dt=F32):
            return ctx.enter_context(nc.sbuf_tensor(name, shape, dt))

        def ps(name, shape):
            return ctx.enter_context(nc.psum_tensor(name, shape, F32))

        def sem(name):
            return ctx.enter_context(nc.semaphore(name))

        x = sb("x", [P, TOK // P, P])
        ident = sb("ident", [P, P])
        arena = sb("arena", [P, ARENA])
        used = [0, 0]

        def part(phase, shape):
            size = int(np.prod(shape[1:]))
            view = arena[0:shape[0], used[phase]:used[phase] + size]
            used[phase] += size
            assert used[phase] <= ARENA, used
            if len(shape) == 3:
                view = view.rearrange("p (a b) -> p a b", a=shape[1])
            if len(shape) == 4:
                view = view.rearrange("p (a b c) -> p a b c", a=shape[1], b=shape[2])
            return view

        w_raw = part(0, [P, NX, 2 * HID + 2 * P])
        up_hi = sb("up_hi", [P, NX, 2 * HID], F32R)
        up_lo = sb("up_lo", [P, NX, 2 * HID], F32R)
        down_hi = sb("down_hi", [P, NX, 2 * P], F32R)
        down_lo = sb("down_lo", [P, NX, 2 * P], F32R)
        rw = sb("rw", [P, NE])
        rb = sb("rb", [P, TT, NE])
        iota = sb("expert_iota", [P, TT, NE])
        pick_f = part(0, [2 * NE, NE, P])
        pick = sb("pick", [2 * NE, NE, P], F32R)
        minus_half = sb("minus_half", [P, TT])
        stats = sb("stats", [P, TT, 6])
        mv = sb("mv", [P, TT, 2])
        var_eps = sb("var_eps", [P, TT])
        rstd = sb("rstd", [P, TT])
        silu_a = part(0, [P, 2, BT])
        xn = part(0, [P, TT, P])
        xt = part(0, [P, BT])
        xt_hi = sb("xt_hi", [P, 2 * BT], F32R)
        xt_lo = sb("xt_lo", [P, 2 * BT], F32R)
        logits = sb("logits", [P, TT, NE])
        top = sb("top", [P, TT, 8])
        top_i = sb("top_i", [P, TT, 8], U32)
        top_f = sb("top_f", [P, TT, 2])
        gap = sb("gap", [P, TT])
        gap_tanh = sb("gap_tanh", [P, TT])
        share = sb("share", [P, 2, TT])
        hot = sb("hot", [P, 2, TT, NE])
        gate = sb("gate", [P, TT, NE])
        gate_parts = sb("gate_parts", [P, TT, 2 * NE])
        gates_t = sb("gates_t", [2 * NE, 2 * BT], F32R)
        gated = part(0, [P, 2, BT])
        hid = part(0, [P, 2, BT])
        hid_hi = sb("hid_hi", [P, 3, BT], F32R)
        hid_lo = sb("hid_lo", [P, 3, BT], F32R)
        half_out = part(0, [P, BT])

        ps_a = ps("ps_a", [P, 2, BT])
        ps_b = ps("ps_b", [P, 2, BT])
        ps_go = ps("ps_go", [P, 2, BT])
        ps_tr = ps("ps_tr", [P, 2, BT])
        ps_g, ps_o = ps_go[:, 0, :], ps_go[:, 1, :]
        ps_t, ps_r = ps_tr[:, 0, :], ps_tr[:, 1, :]

        col = sb("col", [P, NCOL])
        root_a = sb("root_a", [P, 1])
        root_a_inv = sb("root_a_inv", [P, 1])
        pow_in = sb("pow_in", [P, 3])
        w_tap = part(1, [P, TAPS, DI + 2 * DS])
        w_z = part(1, [P, DI])
        w_dt = part(1, [P, P])
        w_out = part(1, [P, 2, P])
        w_gate = part(1, [P, FF])
        w_up = part(1, [P, FF])
        w_down = part(1, [P, FC, P])
        restart = sb("restart", [P, CB, CH], BF16)
        restart_small = sb("restart_small", [P, TT, CT])
        causal = sb("causal", [P, CT, NH, CH], BF16)
        own_head = sb("own_head", [P, DI])
        halo_zero = sb("halo_zero", [P, TAPS - 1])
        zt = part(1, [P, TAPS - 1 + BT])
        zn = part(1, [P, TT, P])
        us = part(1, [P, 2, 2, BT])
        zs = part(1, [P, 2, 2, BT])
        t_all = part(1, [P, 6, BT])
        t0, t1, t2, t3, t4, t5 = (t_all[:, n, :] for n in range(6))
        taps_in = us.rearrange("p a b c -> p (a b c)")[:, 0:TAPS * (DI + 2 * DS)]
        columns_in = zs.rearrange("p a b c -> p (a b c)")[:, 0:IN_COLS]
        cfs = part(1, [P, 2, BT])
        bf = part(1, [P, TT, CT * P])
        cfx = part(1, [P, TT, CT * NH * CH])
        decay = sb("decay", [P, 2, TT, CT * CT + CT + 2])
        amv = sb("amv", [P, 2, TT, 2])
        arstd = sb("arstd", [P, 2, TT])
        phase = sb("phase", [P, 2, CB + 1])
        bc_act = part(1, [P, BT])[0:2 * DS, :]
        bc_rep = part(1, [P, 2 * TT, 2 * NH * DS]).rearrange("p g (r n) -> p g r n", n=DS)
        astats = sb("astats", [P, TT, 6])
        azr = sb("azr", [P, TT])
        asmall = sb("asmall", [P, 4, TT])
        half8 = sb("half8", [P, 2 * TT])
        bc_tm = sb("bc_tm", [P, 2 * TT, DS])
        bc_sq = sb("bc_sq", [P, 2 * TT, DS])
        bc_n = sb("bc_n", [P, 3, 2 * TT])
        ctot = sb("ctot", [P, TT, CT])
        cmid = sb("cmid", [P, TT, CT])
        cinc = sb("cinc", [P, TT, CT])
        refs = sb("refs", [P, TT, CT])
        turns = sb("turns", [P, 3, CB])
        phase_c = sb("phase_c", [P, CB])
        phase_b = sb("phase_b", [P, CB])
        state = sb("state", [P, 2, DI])
        state_new = sb("state_new", [P, DI])
        tm = sb("tm", [P, 2, DI + P])
        gram = sb("gram", [P, 2, CT, NH, CH])
        mo = part(1, [P, BT])
        hb = part(1, [P, TT, P])
        hnt = mo
        hf = part(1, [P, FC, BT])
        hmv = sb("hmv", [P, TT, 2])
        hstats = sb("hstats", [P, TT, 6])
        hsm = sb("hsm", [P, 3, TT])

        pf_c, pf_b = ps_a[:, 0, :], ps_b[:, 0, :]
        pf_uz = (ps_a[:, 1, :], ps_b[:, 1, :])
        pb_ds, pb_o = ps_go[:, 0, :], ps_go[:, 1, :]
        pb_t, pb_gram = ps_tr[:, 0, :], ps_tr[:, 1, :]
        pb_gate = (pb_gram, pb_t, pb_gram)
        pb_up = (pb_o, pb_ds, pb_o)
        pb_down = pb_ds

        carried = sem("carried")
        x_in = [sem(f"x_in{i}") for i in range(2)]
        w_in = [sem(f"w_in{i}") for i in range(3)]
        small_in = sem("small_in")
        out_stored = sem("out_stored")
        pool_const = sem("pool_const")
        pick_ready = sem("pick_ready")
        w_hi_ready = sem("w_hi_ready")
        w_lo_ready = sem("w_lo_ready")
        mv_ready = sem("mv_ready")
        xn_ready = sem("xn_ready")
        xt_ps_ready = sem("xt_ps_ready")
        xt_ready = sem("xt_ready")
        xt_lo_ready = sem("xt_lo_ready")
        logits_ps_ready = sem("logits_ps_ready")
        gap_ready = sem("gap_ready")
        tanh_ready = sem("tanh_ready")
        gates_ready = sem("gates_ready")
        gates_ps_ready = sem("gates_ps_ready")
        gates_t_ready = sem("gates_t_ready")
        a_ps_ready = sem("a_ps_ready")
        b_ps_ready = sem("b_ps_ready")
        g_ps_ready = sem("g_ps_ready")
        silu_done = sem("silu_done")
        gated_done = sem("gated_done")
        hid_done = sem("hid_done")
        hi_done = sem("hi_done")
        lo_done = sem("lo_done")
        down_done = sem("down_done")
        half_out_ready = sem("half_out_ready")
        out_ps_ready = sem("out_ps_ready")
        residual_done = sem("residual_done")
        dve_prep = sem("dve_prep")
        pool_prep = sem("pool_prep")

        wm_in = sem("wm_in")
        conv_in = sem("conv_in")
        col_in = sem("col_in")
        mixer_const = sem("mixer_const")
        mixer_const_act = sem("mixer_const_act")
        mixer_const_dve = sem("mixer_const_dve")
        features_clear = sem("features_clear")
        (amv_ready, arstd_ready, zn_ready, zt_ps_ready, zt_ready, uz_ps_ready, bc_ps_ready, dt_ps_ready, silu_u_done, silu_bc_done, silu_z_done, bct_ps_ready,
         bc_n2_ready, bc_norm_ready, bcn_ready, rep_ps_ready, softplus_parts, dt_ready, theta_ready, theta_max_ready,
         inv_ready, decay_args_ready, decays_ready, decay_big_ready, angle_in_ready, arctan_done, angle_ready,
         turns_ready, phase_c_ready, phase_b_ready, sine_c_done, sine_b_done, cf_ready, cfs_ready, bf_ready, cfx_ready,
         tm_ps_ready, tm_ready, gram_ps_ready, gram_ready, ds_ps_ready, state_ready, o_ps_ready, y_ready,
         mix_f_ps_ready, mix_f_ready, mix_ps_ready, hmv_ready, hr_ready, hn_ready, hnt_ps_ready, hnt_ready,
         gate_ps_ready, up_ps_ready, silu_g_done, hf_ready, ffn_ps_ready, ffn_f_ready, ffn_t_ps_ready, mixer_done,
         oy_ready, chunk_logs_ready, hb_ready, state_clear, own_act, own_dve_pre, own_dve_front, own_dve_back, own_dve_tail, own_pool_pre,
         own_pool_tail, own_pool_refs) = (sem("m_" + n) for n in (
            "amv", "arstd", "zn", "zt_ps", "zt", "uz_ps", "bc_ps", "dt_ps", "silu_u", "silu_bc", "silu_z", "bct_ps", "bc_n2", "bc_norm", "bcn",
            "rep_ps", "softplus", "dt", "theta", "theta_max", "inv", "decay_args", "decays", "decay_big", "angle_in",
            "arctan", "angle", "turns", "phase_c", "phase_b", "sine_c", "sine_b", "cf", "cfs", "bf", "cfx", "tm_ps",
            "tm", "gram_ps", "gram", "ds_ps", "state", "o_ps", "y", "mix_f_ps", "mix_f", "mix_ps", "hmv", "hr", "hn",
            "hnt_ps", "hnt", "gate_ps", "up_ps", "silu_g", "hf", "ffn_ps", "ffn_f", "ffn_t_ps", "mixer_done",
            "oy", "chunk_logs", "hb", "state_clear", "own_act", "own_dve_pre", "own_dve_front", "own_dve_back", "own_dve_tail",
            "own_pool_pre", "own_pool_tail", "own_pool_refs"))

        PREP_DVE = 16
        PREP_POOL = 2

        def after(eng, semaphore, value):
            if not (isinstance(value, int) and value <= 0):
                eng.wait_ge(semaphore, value)

        def in_order(eng, enter, body):
            enter((0, 0))
            body(None, (0, 0), (0, 1))
            body((0, 0), (0, 1), (1, 0))
            body((0, 1), (1, 0), (1, 1))
            with eng.Fori(1, NSEQ - 1) as b:
                body((b, 0), (b, 1), (b + 1, 0))
                body((b, 1), (b + 1, 0), (b + 1, 1))
            body((NSEQ - 1, 0), (NSEQ - 1, 1), None)
            body((NSEQ - 1, 1), None, None)

        MIXER_CONST = 18
        DVE_FRONT = 22
        DVE_BACK = 4

        def apart(eng):
            eng.sem_inc(carried, 1)

        def tiles(blk):
            return bass.ds(blk * TT, TT)

        def half(turn, size=BT):
            if isinstance(turn, int):
                return bass.ds((turn % 2) * size, size)
            return bass.ds((turn & 1) * size, size)

        def first_block(b, q):
            return isinstance(b, int) and SQ * b + q == 0

        def uz_bank(b, q, z, k):
            if first_block(b, q):
                return ((pb_ds, pb_o), (pb_t, pb_gram))[z][k]
            return pf_uz[k]

        def token_bank(turn):
            return ps_b[:, 1, :] if isinstance(turn, int) and turn == NB else ps_t

        def route_bank(turn):
            return ps_a[:, 1, :] if isinstance(turn, int) and turn == NB else ps_r

        block = ctx.enter_context(nc.Block())

        @block.sync
        def _(sp):
            xv = A["L0_attn_x"].rearrange("b (t p) d -> p (b t) d", p=P)
            sp.dma_start(x[:, 0:TT, :], xv[:, 0:TT, :]).then_inc(x_in[0], 16)
            sp.dma_start(rw[:, :], A["L0_ffn_rw"]).then_inc(small_in, 16)
            sp.dma_start(rb[:, :, :], A["L0_ffn_rb"].rearrange("(a b e) -> a b e", a=1, b=1)
                         .broadcast_to([P, TT, NE])).then_inc(small_in, 16)
            sp.dma_start(w_raw[:, 0, 0:HID], A["L0_ffn_sw1"]).then_inc(w_in[0], 16)
            sp.dma_start(w_raw[:, 0, HID:2 * HID], A["L0_ffn_sw2"]).then_inc(w_in[0], 16)
            sp.dma_start(w_raw[:, 0, 2 * HID:].rearrange("p (k d) -> p k d", k=2),
                         A["L0_ffn_sw3"].rearrange("(k p) d -> p k d", p=P)).then_inc(w_in[0], 16)
            sp.dma_start(col[:, :], A["columns"]).then_inc(col_in, 16)
            for n in range(2):
                es = slice(4 * n, 4 * n + 4)
                ws = slice(1 + 4 * n, 5 + 4 * n)
                sp.dma_start(w_raw[:, ws, 0:HID],
                             A["L0_ffn_ew1"][es].rearrange("e d h -> d e h")).then_inc(w_in[1 + n], 16)
                sp.dma_start(w_raw[:, ws, HID:2 * HID],
                             A["L0_ffn_ew2"][es].rearrange("e d h -> d e h")).then_inc(w_in[1 + n], 16)
                for e in range(4 * n, 4 * n + 4):
                    sp.dma_start(w_raw[:, 1 + e, 2 * HID:].rearrange("p (k d) -> p k d", k=2),
                                 A["L0_ffn_ew3"][e].rearrange("(k p) d -> p k d", p=P)).then_inc(w_in[1 + n], 16)
            sp.dma_start(x[:, TT:, :], xv[:, TT:, :]).then_inc(x_in[1], 16)
            sp.wait_ge(w_hi_ready, 2 * NX)
            sp.wait_ge(w_lo_ready, 2 * NX)
            sp.dma_start(taps_in,
                         A["conv_taps"].broadcast_to([P, TAPS * (DI + 2 * DS)])).then_inc(conv_in, 16)
            sp.dma_start(columns_in, A["in_proj_t"]).then_inc(conv_in, 16)
            sp.dma_start(w_z[:, :], A["in_proj_t"][:, 0:DI]).then_inc(wm_in, 16)
            sp.dma_start(w_out[:, :, :], A["out_proj_t"].rearrange("(k p) d -> p k d", p=P)).then_inc(wm_in, 16)
            sp.dma_start(w_gate[:, :], A["gate_t"]).then_inc(wm_in, 16)
            sp.dma_start(w_up[:, :], A["up_t"]).then_inc(wm_in, 16)
            sp.dma_start(w_down[:, 0:2, :], A["down_t"][0:2 * P].rearrange("(k p) d -> p k d", p=P)).then_inc(wm_in, 16)
            sp.dma_start(w_down[0:FF - 2 * P, 2, :], A["down_t"][2 * P:FF]).then_inc(wm_in, 16)
            ov = out.rearrange("b (t p) d -> p (b t) d", p=P)
            for n in range(NB):
                sp.wait_ge(residual_done, NB + n + 1)
                sp.dma_start(ov[:, n * TT:(n + 1) * TT, :], x[:, n * TT:(n + 1) * TT, :]).then_inc(out_stored, 16)
            sp.wait_ge(out_stored, 16 * NB)

        W_LOADS = [48] + [96] * 2

        def weights_loaded(eng, e):
            n = 0 if e == 0 else 1 + (e - 1) // 4
            eng.wait_ge(w_in[n], W_LOADS[n])

        def pool_rstd(pool, turn):
            own = Steps(pool, pool_prep, PREP_POOL, turn)
            pool.wait_ge(mv_ready, turn + 1)
            apart(pool)
            own.step(pool.tensor_scalar(var_eps[:, :], mv[:, :, 1], LN_EPS, None, ALU.add))
            own.settle()
            own.step(pool.tensor_tensor(rstd[:, :], var_eps[:, :], minus_half[:, :], ALU.pow))
            own.close()

        def pool_xt_lo(pool, turn):
            pool.wait_ge(xt_ready, 2 * turn + 2)
            pool.tensor_tensor(xt_lo[:, half(turn)], xt[:, :], xt_hi[:, half(turn)].bitcast(F32),
                               ALU.subtract).then_inc(xt_lo_ready, 1)

        def pool_step(pool, turn, s):
            n = turn * STEPS + s
            pool.wait_ge(hi_done, n + 1)
            if not (isinstance(turn, int) and n < 3):
                pool.wait_ge(down_done, n - 2)
            pool.tensor_tensor(hid_lo[:, s % 3, :], hid[:, s % 2, :], hid_hi[:, s % 3, :].bitcast(F32),
                               ALU.subtract).then_inc(lo_done, 1)

        def pool_block(pool, call, blk, last=False):
            turn = blk + call * NB
            for s in range(STEPS):
                pool_step(pool, turn, s)
                if s == 3 and not last:
                    pool_rstd(pool, turn + 1)
                if s == 4 and last and call == 0:
                    pool_norms(pool, 0, 0)
                if s == 9 and not last:
                    pool_xt_lo(pool, turn + 1)

        def pool_route_const(pool):
            pool.memset(pick_f[:, :, :], 0.0).then_inc(pool_const, 1)
            pool.iota(iota[:, :, :], pattern=[[0, TT], [1, NE]], base=0, channel_multiplier=0,
                      allow_small_or_imprecise_dtypes=True).then_inc(pool_const, 1)
            pool.wait_ge(pool_const, 5)
            pool.affine_select(out=pick_f[:, :, :], in_=pick_f[:, :, :], compare_op=ALU.not_equal, fill=1.0, base=0,
                               pattern=[[-1, NE], [0, P]], channel_multiplier=1).then_inc(pool_const, 1)
            pool.wait_ge(pool_const, 6)
            pool.affine_select(out=pick_f[:, :, :], in_=pick_f[:, :, :], compare_op=ALU.not_equal, fill=1.0, base=-NE,
                               pattern=[[-1, NE], [0, P]], channel_multiplier=1).then_inc(pool_const, 1)

        def pool_ffn(pool, call):
            if call == 0:
                pool_rstd(pool, 0)
                pool_route_const(pool)
                pool_xt_lo(pool, 0)
                pool_mixer_const(pool)
            pool_block(pool, call, 0)
            with pool.Fori(1, NB - 1) as blk:
                pool_block(pool, call, blk)
            pool_block(pool, call, NB - 1, last=True)

        def pool_mixer_const(pool):
            m = mixer_const
            pool.memset(restart[:, :, :], 1.0).then_inc(m, 1)
            pool.memset(restart_small[:, :, :], 1.0).then_inc(m, 1)
            pool.memset(causal[:, :, :, :], 1.0).then_inc(m, 1)
            pool.memset(own_head[:, :], 1.0).then_inc(m, 1)
            pool.memset(halo_zero[:, :], 0.0).then_inc(m, 1)
            pool.memset(gram[:, :, :, :, :], 0.0).then_inc(m, 1)
            pool.memset(half8[:, :], 0.5).then_inc(m, 1)
            pool.memset(phase[:, 0, 0:1], 0.0).then_inc(m, 1)
            pool.memset(pow_in[:, 0:1], float(np.e)).then_inc(m, 1)
            pool.wait_ge(col_in, 16)
            pool.tensor_scalar(pow_in[:, 1:2], col[:, C_ALOG:C_ALOG + 1], 0.5, None, ALU.mult).then_inc(m, 1)
            pool.tensor_scalar(pow_in[:, 2:3], col[:, C_ALOG:C_ALOG + 1], -0.5, None, ALU.mult).then_inc(m, 1)
            pool.wait_ge(m, 11)
            pool.memset(restart[:, :, 0:1], 0.0).then_inc(m, 1)
            pool.memset(restart_small[:, :, 0:1], 0.0).then_inc(m, 1)
            pool.affine_select(out=causal[:, :, :, :], in_=causal[:, :, :, :], compare_op=ALU.is_ge, fill=0.0, base=0,
                               pattern=[[CH, CT], [0, NH], [1, CH]], channel_multiplier=-1).then_inc(m, 1)
            pool.affine_select(out=own_head[:, :], in_=own_head[:, :], compare_op=ALU.is_ge, fill=0.0, base=0,
                               pattern=[[-CH, NH], [0, DH]], channel_multiplier=1).then_inc(m, 1)
            pool.tensor_tensor(root_a[:, :], pow_in[:, 0:1], pow_in[:, 1:2], ALU.pow).then_inc(m, 1)
            pool.tensor_tensor(root_a_inv[:, :], pow_in[:, 0:1], pow_in[:, 2:3], ALU.pow).then_inc(m, 1)
            pool.wait_ge(m, 17)
            pool.affine_select(out=own_head[:, :], in_=own_head[:, :], compare_op=ALU.is_ge, fill=0.0, base=CH - 1,
                               pattern=[[CH, NH], [0, DH]], channel_multiplier=-1).then_inc(m, 1)

        def pool_clear_features(pool):
            pool.wait_ge(residual_done, NB)
            pool.memset(bf, 0.0).then_inc(features_clear, 1)
            pool.memset(cfx, 0.0).then_inc(features_clear, 1)

        def pool_norms(pool, b, q):
            n = SQ * b + q
            own = Steps(pool, own_pool_pre, 6, n)

            def step(instruction):
                own.step(instruction)
                own.settle()

            var = amv[:, q, :, 1]
            pool.wait_ge(amv_ready, n + 1)
            apart(pool)
            step(pool.tensor_scalar(asmall[:, 0, :], var, LN_EPS, None, ALU.add))
            step(pool.tensor_tensor(arstd[:, q, :], asmall[:, 0, :], minus_half[:, :], ALU.pow))
            step(pool.tensor_tensor(asmall[:, 1, :], arstd[:, q, :], arstd[:, q, :], ALU.mult))
            step(pool.tensor_tensor(asmall[:, 2, :], asmall[:, 1, :], var, ALU.mult))
            apart(pool)
            step(pool.tensor_scalar(asmall[:, 3, :], asmall[:, 2, :], RMS_EPS, None, ALU.add))
            step(pool.tensor_tensor(asmall[:, 0, :], asmall[:, 3, :], minus_half[:, :], ALU.pow))
            pool.tensor_tensor(azr[:, :], arstd[:, q, :], asmall[:, 0, :], ALU.mult).then_inc(arstd_ready, 1)
            own.close()

        def pool_mixer(pool):
            def bc_norms(b, q):
                n = SQ * b + q
                pool.wait_ge(bc_n2_ready, n + 1)
                pool.tensor_tensor(bc_n[:, 1, :], bc_n[:, 0, :], half8[:, :], ALU.pow).then_inc(bc_norm_ready, 1)

            def c_places(b, q):
                n = SQ * b + q
                pool.wait_ge(features_clear, 2)
                pool.wait_ge(cf_ready, n + 1)
                apart(pool)
                for h in range(NH):
                    rows = slice(h * CH, (h + 1) * CH)
                    pool.tensor_scalar(cfx[rows].rearrange("p t (j h c) -> p t j h c", j=CT, h=NH)[:, :, :, h, :],
                                       t4[rows].rearrange("p (t j c) -> p t j c", t=TT, j=CT),
                                       1.0, 0.0, ALU.mult, ALU.add).then_inc(cfx_ready, 1)
                pool.wait_ge(cfx_ready, NH * n + NH)

            def log_refs(b, q):
                n = SQ * b + q
                own = Steps(pool, own_pool_refs, 3, n)
                pool.wait_ge(chunk_logs_ready, n + 1)
                own.step(pool.tensor_tensor(refs[:, :, :], cinc[:, :, :], ctot[:, :, :], ALU.subtract))
                own.settle()
                own.step(pool.tensor_tensor(refs[:, :, :], refs[:, :, :], cmid[:, :, :], ALU.add))
                own.settle()
                d = decay[:, q, :, :]
                for j in range(CT):
                    pool.tensor_tensor(d[:, :, j * CT:(j + 1) * CT],
                                       refs[:, :, j:j + 1].broadcast_to([P, TT, CT]), refs[:, :, :], ALU.subtract)
                own.step(pool.tensor_tensor(d[:, :, CT * CT + CT + 1:], cinc[:, :, CT - 1:CT], refs[:, :, CT - 1:CT],
                                            ALU.subtract))
                pool.tensor_scalar(d[:, :, CT * CT:CT * CT + CT], refs[:, :, :], 1.0, 0.0, ALU.mult, ALU.add)
                pool.tensor_scalar(d[:, :, CT * CT + CT:CT * CT + CT + 1], cinc[:, :, CT - 1:CT], 1.0, 0.0, ALU.mult, ALU.add)
                own.settle()
                apart(pool)
                pool.tensor_scalar(d[:, :, 0:CT * CT], d[:, :, 0:CT * CT], 0.0, None,
                                   ALU.max).then_inc(decay_args_ready, 1)
                own.close()

            def tail(b, q):
                n = SQ * b + q
                own = Steps(pool, own_pool_tail, 3, n)

                def step(instruction):
                    own.step(instruction)
                    own.settle()

                pool.wait_ge(hmv_ready, n + 1)
                step(pool.tensor_tensor(hsm[:, 0, :], hmv[:, :, 0], hmv[:, :, 0], ALU.mult))
                step(pool.tensor_tensor(hsm[:, 1, :], hsm[:, 0, :], hmv[:, :, 1], ALU.add))
                apart(pool)
                step(pool.tensor_scalar(hsm[:, 0, :], hsm[:, 1, :], RMS_EPS, None, ALU.add))
                pool.tensor_tensor(hsm[:, 2, :], hsm[:, 0, :], minus_half[:, :], ALU.pow).then_inc(hr_ready, 1)
                own.close()

            def body(now, next, then):
                if then:
                    pool_norms(pool, *then)
                if next:
                    bc_norms(*next)
                    log_refs(*next)
                if now:
                    if not next:
                        pool_rstd(pool, NB)
                        pool_xt_lo(pool, NB)
                    tail(*now)
                if next:
                    c_places(*next)

            in_order(pool, lambda n: pool_clear_features(pool), body)

        @block.gpsimd
        def _(pool):
            pool.memset(ident[:, :], 0.0).then_inc(pool_const, 1)
            pool.memset(minus_half[:, :], -0.5).then_inc(pool_const, 1)
            pool.wait_ge(pool_const, 2)
            pool.affine_select(out=ident[:, :], in_=ident[:, :], compare_op=ALU.not_equal, fill=1.0, base=0,
                               pattern=[[-1, P]], channel_multiplier=1).then_inc(pool_const, 1)
            pool_ffn(pool, 0)
            pool_mixer(pool)
            pool_ffn(pool, 1)

        def act_w_hi(act, e):
            weights_loaded(act, e)
            act.activation(up_hi[:, e, :], w_raw[:, e, 0:2 * HID], ACT.Copy).then_inc(w_hi_ready, 1)
            act.activation(down_hi[:, e, :], w_raw[:, e, 2 * HID:], ACT.Copy).then_inc(w_hi_ready, 1)

        def act_xt(act, turn):
            act.wait_ge(xt_ps_ready, turn + 1)
            act.activation(xt[:, :], token_bank(turn), ACT.Copy).then_inc(xt_ready, 1)
            act.activation(xt_hi[:, half(turn)], token_bank(turn), ACT.Copy).then_inc(xt_ready, 1)

        def act_tanh(act, turn):
            act.wait_ge(gap_ready, turn + 1)
            act.activation(gap_tanh[:, :], gap[:, :], ACT.Tanh, scale=0.5).then_inc(tanh_ready, 1)

        def act_gates(act, turn):
            act.wait_ge(gates_ps_ready, turn + 1)
            act.activation(gates_t[:, half(turn)], route_bank(turn)[0:2 * NE, :], ACT.Copy).then_inc(gates_t_ready, 1)

        def act_half_out(act, turn):
            act.wait_ge(down_done, STEPS * (turn + 1))
            if not (isinstance(turn, int) and turn == 0):
                act.wait_ge(out_ps_ready, turn)
            act.activation(half_out[:, :], ps_o[:, :], ACT.Copy, scale=0.5).then_inc(half_out_ready, 1)

        def act_silu(act, turn, s):
            n = turn * STEPS + s
            act.wait_ge(a_ps_ready, n + 1)
            if not (isinstance(turn, int) and n < 2):
                act.wait_ge(gated_done, n - 1)
            act.activation(silu_a[:, s % 2, :], ps_a[:, s % 2, :], ACT.Silu).then_inc(silu_done, 1)

        def act_hi(act, turn, s):
            n = turn * STEPS + s
            act.wait_ge(hid_done, n + 1)
            if not (isinstance(turn, int) and n < 3):
                act.wait_ge(down_done, n - 2)
            act.activation(hid_hi[:, s % 3, :], hid[:, s % 2, :], ACT.Copy).then_inc(hi_done, 1)

        def act_block(act, call, blk, first=False, last=False):
            turn = blk + call * NB
            for s in range(STEPS):
                if s == LAG and not first:
                    act_half_out(act, turn - 1)
                act_silu(act, turn, s)
                if call == 0 and first and s == 0:
                    act_gates(act, 0)
                if s >= 1:
                    act_hi(act, turn, s - 1)
                if call == 0 and first and s % 2 == 0 and s // 2 + 2 < NX:
                    act_w_hi(act, s // 2 + 2)
                if s == 8 and not last:
                    act_xt(act, turn + 1)
                if s == 12 and not last:
                    act_tanh(act, turn + 1)
                if s == 15 and not last:
                    act_gates(act, turn + 1)
            act_hi(act, turn, STEPS - 1)

        def act_ffn(act, call):
            if call == 0:
                act_xt(act, 0)
                act_w_hi(act, 1)
                act.wait_ge(pool_const, 7)
                act.activation(pick[:, :, :], pick_f[:, :, :], ACT.Copy).then_inc(pick_ready, 1)
                act_tanh(act, 0)
            act_block(act, call, 0, first=True)
            with act.Fori(1, NB - 1) as blk:
                act_block(act, call, blk)
            if call == 0:
                act_mixer_const(act)
            act_block(act, call, NB - 1, last=True)
            act_half_out(act, call * NB + NB - 1)

        def act_mixer_const(act):
            act.wait_ge(conv_in, 32)
            act.activation(w_dt.rearrange("p (h c) -> p h c", h=NH),
                           columns_in[:, IN_COLS - NH:].rearrange("p (h a) -> p h a", a=1).broadcast_to([P, NH, 2 * DS]),
                           ACT.Copy).then_inc(mixer_const_act, 1)

        def act_mixer(act):
            owns = [None]

            def step(instruction):
                owns[0].step(instruction)
                owns[0].settle()

            def zt_copy(b, q):
                n = SQ * b + q
                act.wait_ge(zt_ps_ready, n + 1)
                after(act, dt_ps_ready, n)
                halo = halo_zero[:, :] if q == 0 else zt[:, BT:]
                own = Steps(act, zt_ready, 2, n)
                own.step(act.activation(zt[:, 0:TAPS - 1], halo, ACT.Copy))
                own.settle()
                own.step(act.activation(zt[:, TAPS - 1:], pf_uz[1], ACT.Copy, scale=col[:, C_NORM1:C_NORM1 + 1]))

            def silu_u(b, q, k):
                n = SQ * b + q
                act.wait_ge(uz_ps_ready, 4 * n + k + 1)
                if k == 0:
                    after(act, y_ready, 2 * (n - 1))
                act.activation(us[:, q, k, :], uz_bank(b, q, 0, k), ACT.Silu,
                               bias=col[:, C_CONVB + k:C_CONVB + k + 1]).then_inc(silu_u_done, 1)

            def silu_bc(b, q):
                n = SQ * b + q
                act.wait_ge(bc_ps_ready, n + 1)
                act.activation(bc_act, pf_uz[0][0:2 * DS], ACT.Silu,
                               bias=col[0:2 * DS, C_CONVBC:C_CONVBC + 1]).then_inc(silu_bc_done, 1)

            def silu_z(b, q, k):
                n = SQ * b + q
                act.wait_ge(uz_ps_ready, 4 * n + k + 3)
                if k == 0:
                    after(act, mix_f_ps_ready, n - 1)
                act.activation(zs[:, q, k, :], uz_bank(b, q, 1, k), ACT.Silu).then_inc(silu_z_done, 1)

            def dt_parts(b, q):
                n = SQ * b + q
                owns[0] = Steps(act, own_act, 4, n)
                act.wait_ge(dt_ps_ready, n + 1)
                after(act, bf_ready, n)
                act.activation(t1, pf_uz[1], ACT.Relu, bias=col[:, C_DTB:C_DTB + 1])
                owns[0].step(act.activation(t0, pf_uz[1], ACT.Abs, bias=col[:, C_DTB:C_DTB + 1]))

            def softplus(b, q):
                owns[0].settle()
                step(act.activation(t0, t0, ACT.Exp, scale=-1.0))
                act.activation(t0, t0, ACT.Ln, bias=1.0).then_inc(softplus_parts, 1)

            def theta(b, q):
                n = SQ * b + q
                act.wait_ge(dt_ready, n + 1)
                step(act.activation(t0, t1, ACT.Square, scale=root_a[:, :]))
                act.activation(t2, t1, ACT.Copy, scale=root_a[:, :])
                act.activation(t3, t0, ACT.Ln, bias=1.0).then_inc(theta_ready, 1)

            def inverse(b, q):
                n = SQ * b + q
                act.wait_ge(theta_max_ready, n + 1)
                step(act.activation(t4, t4, ACT.Ln))
                act.activation(t4, t4, ACT.Exp, scale=-0.5).then_inc(inv_ready, 1)
                owns[0].close()

            def decays(b, q):
                n = SQ * b + q
                act.wait_ge(decay_args_ready, n + 1)
                act.activation(decay[:, q, :, :], decay[:, q, :, :], ACT.Exp, scale=-0.5).then_inc(decays_ready, 1)
                act.wait_ge(decay_big_ready, n + 1)
                act.activation(cfs[:, q, :], cfs[:, q, :], ACT.Exp, scale=-0.5).then_inc(decays_ready, 1)
                act.activation(t3, t3, ACT.Exp, scale=0.5).then_inc(decays_ready, 1)

            def arctan(b, q):
                n = SQ * b + q
                act.wait_ge(angle_in_ready, n + 1)
                act.activation(t2, t2, ACT.Arctan).then_inc(arctan_done, 1)

            def to_turns(b, q):
                n = SQ * b + q
                act.wait_ge(angle_ready, n + 1)
                act.activation(t2, t2, ACT.Abs, scale=float(1 / (2 * np.pi))).then_inc(turns_ready, 1)

            def sine_c(b, q):
                n = SQ * b + q
                act.wait_ge(phase_c_ready, n + 1)
                act.activation(t4, t4, ACT.Sin, scale=TWO_PI).then_inc(sine_c_done, 1)

            def sine_b(b, q):
                n = SQ * b + q
                act.wait_ge(phase_b_ready, n + 1)
                act.activation(t0, t0, ACT.Sin, scale=TWO_PI).then_inc(sine_b_done, 1)

            def tm_copy(b, q, k):
                act.wait_ge(tm_ps_ready, TT * (SQ * b + q) + k + 1)
                act.activation(tm[:, k % 2, :], pb_t[:, 0:DI + P], ACT.Copy).then_inc(tm_ready, 1)

            def mix_copy(b, q):
                n = SQ * b + q
                act.wait_ge(mix_f_ps_ready, n + 1)
                act.activation(mo, pb_ds, ACT.Copy).then_inc(mix_f_ready, 1)

            def hnt_copy(b, q):
                n = SQ * b + q
                act.wait_ge(hnt_ps_ready, n + 1)
                act.activation(hnt, pb_t, ACT.Copy, scale=col[:, C_NORM2:C_NORM2 + 1]).then_inc(hnt_ready, 1)

            def silu_gate(b, q, c):
                n = SQ * b + q
                rows = slice(0, min(P, FF - c * P))
                act.wait_ge(gate_ps_ready, FC * n + c + 1)
                act.activation(hf[rows, c, :], pb_gate[c][rows], ACT.Silu).then_inc(silu_g_done, 1)

            def ffn_copy(b, q):
                n = SQ * b + q
                act.wait_ge(ffn_ps_ready, n + 1)
                act.activation(mo, pb_down, ACT.Copy).then_inc(ffn_f_ready, 1)

            def body(now, next, then):
                if now and next:
                    dt_parts(*next)
                if now:
                    tm_copy(*now, 1)
                if now and next:
                    softplus(*next)
                if now:
                    tm_copy(*now, 2)
                if now and next:
                    theta(*next)
                if now:
                    tm_copy(*now, 3)
                if now and not next:
                    act_xt(act, NB)
                if then:
                    zt_copy(*then)
                if next:
                    inverse(*next)
                    arctan(*next)
                if then:
                    silu_u(*then, 0)
                if next:
                    to_turns(*next)
                if now:
                    mix_copy(*now)
                if now and not next:
                    act_tanh(act, NB)
                if then:
                    silu_u(*then, 1)
                    silu_z(*then, 0)
                    silu_z(*then, 1)
                if next:
                    decays(*next)
                if now:
                    hnt_copy(*now)
                    silu_gate(*now, 0)
                if next:
                    sine_c(*next)
                    sine_b(*next)
                if now:
                    silu_gate(*now, 1)
                if now and not next:
                    act_gates(act, NB)
                if then:
                    silu_bc(*then)
                if now:
                    silu_gate(*now, 2)
                    ffn_copy(*now)
                if next:
                    tm_copy(*next, 0)

            def enter(n):
                zt_copy(*n)
                dt_parts(*n)
                silu_bc(*n)
                softplus(*n)
                theta(*n)
                silu_u(*n, 0)
                silu_u(*n, 1)
                silu_z(*n, 0)
                silu_z(*n, 1)

            in_order(act, enter, body)

        @block.scalar
        def _(act):
            act_w_hi(act, 0)
            act_ffn(act, 0)
            act.wait_ge(mixer_const, MIXER_CONST)
            act_mixer(act)
            act_ffn(act, 1)

        def dve_w_lo(dve, e):
            weights_loaded(dve, e)
            dve.wait_ge(w_hi_ready, 2 * e + 2)
            dve.tensor_tensor(up_lo[:, e, :], w_raw[:, e, 0:2 * HID], up_hi[:, e, :].bitcast(F32),
                              ALU.subtract).then_inc(w_lo_ready, 1)
            dve.tensor_tensor(down_lo[:, e, :], w_raw[:, e, 2 * HID:], down_hi[:, e, :].bitcast(F32),
                              ALU.subtract).then_inc(w_lo_ready, 1)

        def dve_stats(dve, own, call, blk):
            turn = blk + call * NB
            for t in range(TT):
                own.step(dve.bn_stats(stats[:, t, :], x[:, bass.ds(blk * TT + t, 1), :]))
            own.settle()
            apart(dve)
            for t in range(TT):
                r = dve.bn_aggr(mv[:, t, :], stats[:, t, :])
            r.then_inc(mv_ready, 1)

        def dve_norm(dve, call, blk):
            turn = blk + call * NB
            dve.wait_ge(mv_ready, turn + 1)
            dve.wait_ge(pool_prep, PREP_POOL * (turn + 1))
            if not (isinstance(turn, int) and turn == 0):
                dve.wait_ge(xt_ps_ready, turn)
            for t in range(TT):
                r = dve.tensor_scalar(xn[:, t, :], x[:, bass.ds(blk * TT + t, 1), :], mv[:, t, 0:1], rstd[:, t:t + 1],
                                      ALU.subtract, ALU.mult)
            r.then_inc(xn_ready, 1)

        def dve_route(dve, own, turn):
            dve.wait_ge(logits_ps_ready, turn + 1)
            own.step(dve.tensor_tensor(logits[:, :, :], route_bank(turn)[:, 0:TT * NE].rearrange("p (t e) -> p t e", t=TT),
                                       rb[:, :, :], ALU.add))
            own.settle()
            apart(dve)
            for t in range(TT):
                r = dve.max(top[:, t, :], logits[:, t, :])
            own.step(r)
            own.settle()
            dve.tensor_tensor(gap[:, :], top[:, :, 0], top[:, :, 1], ALU.subtract).then_inc(gap_ready, 1)
            for t in range(TT):
                r = dve.max_index(top_i[:, t, :], top[:, t, :], logits[:, t, :])
            own.step(r)
            own.settle()
            own.step(dve.tensor_copy(top_f[:, :, :], top_i[:, :, 0:2]))
            own.settle()
            for k in range(2):
                own.step(dve.tensor_tensor(hot[:, k, :, :], iota[:, :, :],
                                           top_f[:, :, k:k + 1].broadcast_to([P, TT, NE]), ALU.is_equal))

        def dve_gates(dve, own, turn):
            dve.wait_ge(tanh_ready, turn + 1)
            own.step(dve.tensor_scalar(share[:, 0, :], gap_tanh[:, :], 0.5, 0.5, ALU.mult, ALU.add))
            own.step(dve.tensor_scalar(share[:, 1, :], gap_tanh[:, :], -0.5, 0.5, ALU.mult, ALU.add))
            own.settle()
            for k in range(2):
                own.step(dve.tensor_tensor(hot[:, k, :, :], hot[:, k, :, :],
                                           share[:, k, :].rearrange("p (t a) -> p t a", a=1).broadcast_to([P, TT, NE]),
                                           ALU.mult))
            own.settle()
            own.step(dve.tensor_tensor(gate[:, :, :], hot[:, 0, :, :], hot[:, 1, :, :], ALU.add))
            own.settle()
            if not (isinstance(turn, int) and turn == 0):
                dve.wait_ge(gates_ps_ready, turn)
            own.step(dve.tensor_copy(gate_parts[:, :, 0:NE].bitcast(F32R), gate[:, :, :]))
            own.settle()
            dve.tensor_tensor(gate_parts[:, :, NE:], gate[:, :, :], gate_parts[:, :, 0:NE],
                              ALU.subtract).then_inc(gates_ready, 1)

        def dve_residual(dve, call, blk):
            turn = blk + call * NB
            dve.wait_ge(out_ps_ready, turn + 1)
            dve.tensor_tensor(x[:, tiles(blk), :], x[:, tiles(blk), :],
                              ps_t[:, :].rearrange("p (t d) -> p t d", t=TT), ALU.add).then_inc(residual_done, 1)

        def dve_step(dve, turn, s):
            n = turn * STEPS + s
            dve.wait_ge(silu_done, n + 1)
            if s < 2:
                source, done = silu_a[:, s % 2, :], None
            else:
                if s % 2 == 0:
                    dve.wait_ge(g_ps_ready, turn * NE + s // 2)
                dve.tensor_tensor(gated[:, s % 2, :], silu_a[:, s % 2, :], ps_g[:, :], ALU.mult).then_inc(gated_done, 1)
                dve.wait_ge(gated_done, n + 1)
                source = gated[:, s % 2, :]
            dve.wait_ge(b_ps_ready, n + 1)
            if not (isinstance(turn, int) and n < 2):
                dve.wait_ge(hi_done, n - 1)
                dve.wait_ge(lo_done, n - 1)
            r = dve.tensor_tensor(hid[:, s % 2, :], source, ps_b[:, s % 2, :], ALU.mult)
            r.then_inc(hid_done, 1)
            if s < 2:
                dve.wait_ge(hid_done, n + 1)
                dve.sem_inc(gated_done, 1)

        def dve_block(dve, call, blk, first=False, last=False):
            turn = blk + call * NB
            own = Steps(dve, dve_prep, PREP_DVE, turn + 1)
            for s in range(STEPS):
                dve_step(dve, turn, s)
                if call == 0 and first and s % 2 == 0 and s // 2 + 2 < NX:
                    dve_w_lo(dve, s // 2 + 2)
                if s == 3 and not last:
                    if call == 0 and first:
                        dve.wait_ge(x_in[1], 16)
                    dve_stats(dve, own, call, blk + 1)
                if s == 3 and last and call == 0:
                    dve_mixer_stats(dve, 0, 0)
                if s == 4 and not first:
                    dve_residual(dve, call, blk - 1)
                if s == 6 and last and call == 0:
                    dve_mixer_norm(dve, 0, 0)
                if s == 6 and not last:
                    dve_norm(dve, call, blk + 1)
                if s == 11 and not last:
                    dve_route(dve, own, turn + 1)
                if s == 13 and not last:
                    dve_gates(dve, own, turn + 1)
            if not last:
                own.close()

        def dve_ffn(dve, call):
            if call == 0:
                own = Steps(dve, dve_prep, PREP_DVE, 0)
                dve_stats(dve, own, 0, 0)
                dve_norm(dve, 0, 0)
                dve_w_lo(dve, 0)
                dve.wait_ge(small_in, 32)
                dve.wait_ge(pool_const, 5)
                dve_route(dve, own, 0)
                dve_gates(dve, own, 0)
                own.close()
                dve_w_lo(dve, 1)
            dve_block(dve, call, 0, first=True)
            with dve.Fori(1, NB - 1) as blk:
                dve_block(dve, call, blk)
            if call == 0:
                dve_mixer_const(dve)
            dve_block(dve, call, NB - 1, last=True)
            dve_residual(dve, call, NB - 1)

        def dve_mixer_const(dve):
            dve.wait_ge(conv_in, 32)
            for k in range(TAPS):
                r = dve.tensor_tensor(w_tap[:, k, :], taps_in.rearrange("p (k c) -> p k c", k=TAPS)[:, k, :],
                                      columns_in[:, DI:2 * DI + 2 * DS], ALU.mult)
            r.then_inc(mixer_const_dve, 1)

        def x_tile(b, q, t):
            return x[:, bass.ds(b * SQ * TT + q * TT + t, 1), :]

        def dve_mixer_stats(dve, b, q):
            n = SQ * b + q
            own = Steps(dve, own_dve_pre, 1, n)
            for t in range(TT):
                r = dve.bn_stats(astats[:, t, :], x_tile(b, q, t))
            own.step(r)
            own.settle()
            apart(dve)
            for t in range(TT):
                r = dve.bn_aggr(amv[:, q, t, :], astats[:, t, :])
            r.then_inc(amv_ready, 1)

        def dve_mixer_norm(dve, b, q):
            n = SQ * b + q
            dve.wait_ge(amv_ready, n + 1)
            dve.wait_ge(arstd_ready, n + 1)
            after(dve, zt_ps_ready, n)
            for t in range(TT):
                r = dve.tensor_scalar(zn[:, t, :], x_tile(b, q, t), amv[:, q, t, 0:1], azr[:, t:t + 1],
                                      ALU.subtract, ALU.mult)
            r.then_inc(zn_ready, 1)

        def dve_mixer(dve):
            owns = [None]

            def step(instruction):
                owns[0].step(instruction)
                owns[0].settle()

            def chunks(t):
                return t.rearrange("p (c n) -> p c n", c=CB)

            def tile_chunks(t):
                return t.rearrange("p (t j c) -> p t j c", t=TT, j=CT)

            def flat(small):
                return small[:, :, :].rearrange("p t j -> p (t j)")

            def spread(small):
                return small.rearrange("p (c a) -> p c a", a=1).broadcast_to([P, CB, CH])

            def x_block(b, q):
                return x[:, bass.ds(b * SQ * TT + q * TT, TT), :]

            def bc_squares(b, q):
                n = SQ * b + q
                owns[0] = Steps(dve, own_dve_front, DVE_FRONT, n)
                dve.wait_ge(bct_ps_ready, n + 1)
                step(dve.tensor_copy(bc_tm[:, :, :], pf_uz[0][:, 0:2 * TT * DS].rearrange("p (g n) -> p g n", n=DS)))
                step(dve.tensor_tensor(bc_sq[:, :, :], bc_tm[:, :, :], bc_tm[:, :, :], ALU.mult))
                dve.reduce_sum(bc_n[:, 0, :], bc_sq[:, :, :], axis=mybir.AxisListType.X).then_inc(bc_n2_ready, 1)

            def bc_normed(b, q):
                n = SQ * b + q
                dve.wait_ge(bc_norm_ready, n + 1)
                after(dve, rep_ps_ready, n)
                step(dve.tensor_scalar(bc_n[:, 2, :], bc_n[:, 1, :], RMS_EPS, None, ALU.add))
                step(dve.reciprocal(bc_n[:, 0, :], bc_n[:, 2, :]))
                shape = [P, 2 * TT, 2 * NH, DS]
                dve.tensor_tensor(bc_rep, bc_tm[:, :, :].rearrange("p g (a n) -> p g a n", a=1).broadcast_to(shape),
                                  bc_n[:, 0, :].rearrange("p (g a b) -> p g a b", a=1, b=1).broadcast_to(shape),
                                  ALU.mult).then_inc(bcn_ready, 1)

            def dt_sum(b, q):
                n = SQ * b + q
                dve.wait_ge(softplus_parts, n + 1)
                dve.tensor_tensor(t1, t0, t1, ALU.add).then_inc(dt_ready, 1)

            def theta_max(b, q):
                n = SQ * b + q
                dve.wait_ge(theta_ready, n + 1)
                after(dve, cfx_ready, NH * n)
                dve.tensor_scalar(t4, t0, 1.0, None, ALU.max).then_inc(theta_max_ready, 1)
                dve.tensor_scalar(t0, t0, 1.0, float(-np.pi / 2), ALU.is_gt, ALU.mult)

            def log_sums(b, q):
                n = SQ * b + q
                step(dve.tensor_tensor_scan(t5, restart[:, :, :].rearrange("p c n -> p (c n)"), t3, 0.0,
                                            ALU.mult, ALU.add))
                after(dve, decay_args_ready, n)
                dve.tensor_copy(flat(ctot), chunks(t5)[:, :, CH - 1])
                step(dve.tensor_copy(flat(cmid), chunks(t5)[:, :, CH // 2 - 1]))
                dve.tensor_tensor_scan(flat(cinc), flat(restart_small), flat(ctot), 0.0, ALU.mult,
                                       ALU.add).then_inc(chunk_logs_ready, 1)
                step(dve.tensor_tensor(chunks(t5), chunks(t5), spread(flat(cmid)), ALU.subtract))
                step(dve.tensor_tensor(t3, t5, t3, ALU.subtract))
                dve.tensor_scalar(cfs[:, q, :], t5, -CLAMP, None, ALU.max)
                dve.tensor_scalar(t3, t3, CLAMP, None, ALU.min).then_inc(decay_big_ready, 1)

            def angle_in(b, q):
                dve.wait_ge(inv_ready, SQ * b + q + 1)
                dve.tensor_tensor(t2, t2, t4, ALU.min).then_inc(angle_in_ready, 1)

            def angle(b, q):
                dve.wait_ge(arctan_done, SQ * b + q + 1)
                dve.tensor_tensor(t2, t2, t0, ALU.add).then_inc(angle_ready, 1)

            def phase_sums(b, q):
                n = SQ * b + q
                dve.wait_ge(turns_ready, n + 1)
                step(dve.tensor_tensor_scan(t0, restart[:, :, :].rearrange("p c n -> p (c n)"), t2, 0.0,
                                            ALU.mult, ALU.add))
                step(dve.tensor_copy(turns[:, 0, :], chunks(t0)[:, :, CH - 1]))
                step(dve.tensor_scalar(turns[:, 1, :], turns[:, 0, :], ROUND, -ROUND, ALU.add, ALU.add))
                step(dve.tensor_tensor(turns[:, 2, :], turns[:, 0, :], turns[:, 1, :], ALU.subtract))
                start = 0.0
                if q == 1:
                    start = phase[:, 0, CB:CB + 1]
                    dve.tensor_copy(phase[:, 1, 0:1], start)
                step(dve.tensor_tensor_scan(phase[:, q, 1:], turns[:, 2, :], turns[:, 2, :], start,
                                            ALU.add, ALU.bypass))
                dve.tensor_scalar(phase_c[:, :], phase[:, q, 0:CB], col[:, C_OFFC:C_OFFC + 1], None, ALU.add)
                step(dve.tensor_scalar(phase_b[:, :], phase[:, q, 0:CB], col[:, C_OFFB:C_OFFB + 1], None, ALU.add))

            def sine_args_c(b, q):
                n = SQ * b + q
                step(dve.tensor_tensor(chunks(t4), chunks(t0), spread(phase_c[:, :]), ALU.add))
                dve.tensor_scalar(t5, t4, ROUND, -ROUND, ALU.add, ALU.add)
                step(dve.tensor_tensor(t0, t0, t2, ALU.subtract))
                dve.tensor_tensor(t4, t4, t5, ALU.subtract).then_inc(phase_c_ready, 1)

            def sine_args_b(b, q):
                step(dve.tensor_tensor(chunks(t0), chunks(t0), spread(phase_b[:, :]), ALU.add))
                step(dve.tensor_scalar(t5, t0, ROUND, -ROUND, ALU.add, ALU.add))
                dve.tensor_tensor(t0, t0, t5, ALU.subtract).then_inc(phase_b_ready, 1)

            def c_features(b, q):
                n = SQ * b + q
                dve.wait_ge(rep_ps_ready, n + 1)
                dve.wait_ge(sine_c_done, n + 1)
                dve.wait_ge(decays_ready, 3 * n + 3)
                step(dve.scalar_tensor_tensor(t4, t4, root_a_inv[:, :], pf_c, ALU.mult, ALU.mult))
                dve.tensor_tensor(t4, t4, cfs[:, q, :], ALU.mult).then_inc(cf_ready, 1)

            def b_features(b, q):
                n = SQ * b + q
                dve.wait_ge(sine_b_done, n + 1)
                step(dve.tensor_tensor(t0, t0, pf_b, ALU.mult))
                step(dve.tensor_tensor(t0, t0, t1, ALU.mult))

            def b_diagonal(b, q):
                dve.wait_ge(features_clear, 1)
                slot = bf
                diagonal = bass.AP(slot.tensor, slot.offset, [slot.ap[0], [CT * P, TT], [P + CH, CT], [1, CH]])
                step(dve.tensor_tensor(diagonal, tile_chunks(t0), tile_chunks(t3), ALU.mult))

            def b_between(b, q):
                slot = bf
                diagonal = bass.AP(slot.tensor, slot.offset, [slot.ap[0], [CT * P, TT], [P + CH, CT], [1, CH]])
                for j in range(1, CT):
                    between = decay[:, q, :, j * CT:j * CT + j].rearrange("p t (i a) -> p t i a", a=1)
                    r = dve.tensor_tensor(slot[:, :, j * P:j * P + j * CH].rearrange("p t (i c) -> p t i c", i=j),
                                          diagonal[:, :, 0:j, :], between.broadcast_to([P, TT, j, CH]), ALU.mult)
                r.then_inc(bf_ready, 1)

            def c_relative(b, q):
                n = SQ * b + q
                dve.wait_ge(cf_ready, n + 1)
                to_chunk = decay[:, q, :, CT * CT:CT * CT + CT].rearrange("p t (j a) -> p t j a", a=1)
                dve.tensor_tensor(tile_chunks(cfs[:, q, :]), tile_chunks(t4), to_chunk.broadcast_to([P, TT, CT, CH]),
                                  ALU.mult).then_inc(cfs_ready, 1)
                owns[0].close()

            back = [None]

            def h_start(b, q):
                n = SQ * b + q
                after(dve, hnt_ps_ready, n)
                for t in range(TT):
                    r = dve.tensor_scalar(hb[:, t, :], x_tile(b, q, t), amv[:, q, t, 0:1], arstd[:, q, t:t + 1],
                                          ALU.subtract, ALU.mult)
                r.then_inc(hb_ready, 1)

            def state_start(b, q):
                if q == 0:
                    after(dve, state_ready, TT * (SQ * b + q))
                    dve.memset(state[:, 0, :], 0.0).then_inc(state_clear, 1)

            def gram_copy(b, q, k):
                dve.wait_ge(gram_ps_ready, TT * (SQ * b + q) + k + 1)
                apart(dve)
                dve.copy_predicated(gram[:, k % 2].rearrange("p j h c -> p (j h c)"),
                                    causal[:, :, :, :].rearrange("p j h c -> p (j h c)").bitcast(I16),
                                    pb_gram).then_inc(gram_ready, 1)

            def state_update(b, q, k):
                tile = TT * (SQ * b + q) + k
                if k == 0:
                    back[0] = Steps(dve, own_dve_back, DVE_BACK, SQ * b + q)
                    if q == 0:
                        dve.wait_ge(state_clear, b + 1)
                dve.wait_ge(ds_ps_ready, tile + 1)
                last = CT * CT + CT
                back[0].step(dve.scalar_tensor_tensor(state_new[:, :], pb_ds[:, 0:DI], decay[:, q, k, last + 1:last + 2],
                                                      own_head[:, :], ALU.mult, ALU.mult))
                back[0].settle()
                if k or q:
                    dve.wait_ge(o_ps_ready, tile)
                dve.scalar_tensor_tensor(state[:, (k + 1) % 2, :], state[:, k % 2, :], decay[:, q, k, last:last + 1],
                                         state_new[:, :], ALU.mult, ALU.add).then_inc(state_ready, 1)

            def outputs(b, q, i):
                n = SQ * b + q
                dve.wait_ge(o_ps_ready, TT * n + 2 * i + 2)
                at = slice(2 * i * P, 2 * (i + 1) * P)
                for k in range(2):
                    r = dve.scalar_tensor_tensor(us[:, q, k, at], us[:, q, k, at], col[:, C_D + k:C_D + k + 1],
                                                 pb_o[:, k * 2 * P:(k + 1) * 2 * P], ALU.mult, ALU.add)
                r.then_inc(oy_ready, 1)

            def gated_output(b, q, i):
                n = SQ * b + q
                at = slice(2 * i * P, 2 * (i + 1) * P)
                dve.wait_ge(oy_ready, 2 * n + i + 1)
                dve.tensor_tensor(zs[:, q, :, at], zs[:, q, :, at], us[:, q, :, at], ALU.mult).then_inc(y_ready, 1)
                if i == 1:
                    back[0].close()

            def mixed(b, q):
                n = SQ * b + q
                own = Steps(dve, own_dve_tail, 3, n)
                dve.wait_ge(hb_ready, n + 1)
                dve.wait_ge(mix_ps_ready, n + 1)
                own.step(dve.tensor_tensor(hb, hb, pb_t.rearrange("p (t d) -> p t d", t=TT), ALU.add))
                own.settle()
                for t in range(TT):
                    r = dve.bn_stats(hstats[:, t, :], hb[:, t, :])
                own.step(r)
                own.step(dve.tensor_tensor(x_block(b, q), x_block(b, q), hb, ALU.add))
                own.settle()
                apart(dve)
                for t in range(TT):
                    r = dve.bn_aggr(hmv[:, t, :], hstats[:, t, :])
                r.then_inc(hmv_ready, 1)
                own.close()

            def h_norm(b, q):
                n = SQ * b + q
                dve.wait_ge(hr_ready, n + 1)
                for t in range(TT):
                    r = dve.tensor_scalar(hb[:, t, :], hb[:, t, :], hsm[:, 2, t:t + 1], None, ALU.mult)
                r.then_inc(hn_ready, 1)

            def ffn_hidden(b, q, c):
                n = SQ * b + q
                rows = slice(0, min(P, FF - c * P))
                dve.wait_ge(up_ps_ready, FC * n + c + 1)
                dve.wait_ge(silu_g_done, FC * n + c + 1)
                if c == 0:
                    after(dve, ffn_ps_ready, n)
                dve.tensor_tensor(hf[rows, c, :], hf[rows, c, :], pb_up[c][rows], ALU.mult).then_inc(hf_ready, 1)

            def ffn_add(b, q):
                dve.wait_ge(ffn_t_ps_ready, SQ * b + q + 1)
                dve.tensor_tensor(x_block(b, q), x_block(b, q), pb_o.rearrange("p (t d) -> p t d", t=TT),
                                  ALU.add).then_inc(mixer_done, 1)

            def body(now, next, then):
                if now:
                    gram_copy(*now, 1)
                if then:
                    dve_mixer_stats(dve, *then)
                if now:
                    state_update(*now, 0)
                if now and not next:
                    prep = Steps(dve, dve_prep, PREP_DVE, NB)
                    dve.wait_ge(mixer_done, 1)
                    dve_stats(dve, prep, 1, 0)
                if next:
                    dt_sum(*next)
                    bc_squares(*next)
                if now:
                    gram_copy(*now, 2)
                    state_update(*now, 1)
                    outputs(*now, 0)
                if then:
                    dve_mixer_norm(dve, *then)
                if now:
                    gated_output(*now, 0)
                if now and not next:
                    dve_norm(dve, 1, 0)
                if next:
                    bc_normed(*next)
                if now:
                    gram_copy(*now, 3)
                if next:
                    theta_max(*next)
                if now:
                    state_update(*now, 2)
                if next:
                    angle_in(*next)
                if now:
                    state_update(*now, 3)
                    outputs(*now, 1)
                    gated_output(*now, 1)
                if next:
                    state_start(*next)
                if next:
                    angle(*next)
                    log_sums(*next)
                if now:
                    mixed(*now)
                if now and not next:
                    dve_route(dve, prep, NB)
                if next:
                    phase_sums(*next)
                if now:
                    h_norm(*now)
                if now and not next:
                    dve_gates(dve, prep, NB)
                    prep.close()
                if next:
                    sine_args_c(*next)
                    sine_args_b(*next)
                if now:
                    ffn_hidden(*now, 0)
                if next:
                    c_features(*next)
                if now:
                    ffn_hidden(*now, 1)
                if next:
                    b_features(*next)
                if now:
                    ffn_hidden(*now, 2)
                if next:
                    b_diagonal(*next)
                    b_between(*next)
                    gram_copy(*next, 0)
                if now:
                    ffn_add(*now)
                if next:
                    c_relative(*next)
                    h_start(*next)

            def enter(n):
                dve.wait_ge(mixer_const, MIXER_CONST)
                dve.wait_ge(residual_done, NB)

            in_order(dve, enter, body)

        @block.vector
        def _(dve):
            dve.wait_ge(x_in[0], 16)
            dve_ffn(dve, 0)
            dve_mixer(dve)
            dve.wait_ge(mixer_done, NB)
            dve_ffn(dve, 1)

        def pe_xt(pe, turn):
            pe.wait_ge(xn_ready, turn + 1)
            if not (isinstance(turn, int) and turn < 1):
                pe.wait_ge(xt_ready, 2 * turn)
            if isinstance(turn, int) and turn % NB == 0:
                if turn > 0:
                    pe.wait_ge(residual_done, turn)
            elif not (isinstance(turn, int) and turn < 2):
                pe.wait_ge(residual_done, turn - 1)
            for t in range(TT):
                r = pe.transpose(token_bank(turn)[:, t * P:(t + 1) * P], xn[:, t, :], ident[:, :])
            r.then_inc(xt_ps_ready, 1)

        def pe_logits(pe, turn):
            pe.wait_ge(xt_ready, 2 * turn + 1)
            if not (isinstance(turn, int) and turn < 1):
                pe.wait_ge(gates_t_ready, turn)
            for t in range(TT):
                r = pe.matmul(route_bank(turn)[:, t * NE:(t + 1) * NE], xt[:, t * P:(t + 1) * P], rw[:, :], start=True, stop=True)
            r.then_inc(logits_ps_ready, 1)

        def pe_gates(pe, turn):
            pe.wait_ge(gates_ready, turn + 1)
            apart(pe)
            for t in range(TT):
                r = pe.transpose(route_bank(turn)[0:2 * NE, t * P:(t + 1) * P], gate_parts[:, t, :], ident[:, :])
            r.then_inc(gates_ps_ready, 1)

        def pe_out(pe, turn):
            pe.wait_ge(half_out_ready, turn + 1)
            if not (isinstance(turn, int) and turn >= 0 and (turn + 1) % NB == 0):
                pe.wait_ge(xt_ready, 2 * turn + 4)
            for t in range(TT):
                r = pe.transpose(ps_t[:, t * P:(t + 1) * P], half_out[:, t * P:(t + 1) * P], ident[:, :])
            r.then_inc(out_ps_ready, 1)

        def pe_up(pe, turn, s):
            n = turn * STEPS + s
            e, k = s // 2, s % 2
            if not (isinstance(turn, int) and n < 2):
                pe.wait_ge(silu_done, n - 1)
                pe.wait_ge(hid_done, n - 1)
            for target, ready, at in ((ps_a, a_ps_ready, k * P), (ps_b, b_ps_ready, HID + k * P)):
                pe.matmul(target[:, s % 2, :], up_hi[:, e, at:at + P], xt_hi[:, half(turn)], start=True, stop=False)
                pe.matmul(target[:, s % 2, :], up_hi[:, e, at:at + P], xt_lo[:, half(turn)], start=False, stop=False)
                pe.matmul(target[:, s % 2, :], up_lo[:, e, at:at + P], xt_hi[:, half(turn)], start=False,
                          stop=True).then_inc(ready, 1)
            if s >= 2 and k == 0:
                pe.wait_ge(gated_done, n)
                apart(pe)
                pe.matmul(ps_g[:, :], pick[:, e - 1, :], gates_t[:, half(turn)], start=True,
                          stop=True).then_inc(g_ps_ready, 1)

        def pe_down(pe, turn, s):
            n = turn * STEPS + s
            e, at = s // 2, (s % 2) * P
            pe.wait_ge(lo_done, n + 1)
            if s == 0 and not (isinstance(turn, int) and turn == 0):
                pe.wait_ge(half_out_ready, turn)
            pe.matmul(ps_o[:, :], down_hi[:, e, at:at + P], hid_hi[:, s % 3, :], start=(s == 0), stop=False)
            pe.matmul(ps_o[:, :], down_hi[:, e, at:at + P], hid_lo[:, s % 3, :], start=False, stop=False)
            r = pe.matmul(ps_o[:, :], down_lo[:, e, at:at + P], hid_hi[:, s % 3, :], start=False, stop=(s == STEPS - 1))
            r.then_inc(down_done, 1)

        def pe_block(pe, call, blk, first=False, last=False):
            turn = blk + call * NB
            pe.wait_ge(xt_lo_ready, turn + 1)
            if not (call == 0 and first):
                pe.wait_ge(gates_t_ready, turn + 1)
            for s in range(STEPS):
                if call == 0 and first and s == 2:
                    pe_gates(pe, 0)
                    pe.wait_ge(gates_t_ready, 1)
                    pe.wait_ge(pick_ready, 1)
                if call == 0 and first and s % 2 == 0:
                    pe.wait_ge(w_lo_ready, s + 2)
                if not (call == 1 and first and s == 0):
                    pe_up(pe, turn, s)
                if s >= LAG:
                    pe_down(pe, turn, s - LAG)
                elif not first:
                    pe_down(pe, turn - 1, s - LAG + STEPS)
                if s == 3 and not first:
                    pe_out(pe, turn - 1)
                if s == 7 and not last:
                    pe_xt(pe, turn + 1)
                if s == 10 and not last:
                    pe_logits(pe, turn + 1)
                if s == 14 and not last:
                    pe_gates(pe, turn + 1)

        def pe_ffn(pe, call):
            if call == 0:
                pe_xt(pe, 0)
                pe_logits(pe, 0)
            else:
                pe.wait_ge(mixer_done, NB)
            pe_block(pe, call, 0, first=True)
            with pe.Fori(1, NB - 1) as blk:
                pe_block(pe, call, blk)
            pe_block(pe, call, NB - 1, last=True)
            end = call * NB + NB - 1
            for s in range(STEPS - LAG, STEPS):
                pe_down(pe, end, s)
            pe_out(pe, end)

        def pe_mixer_const(pe):
            pe.wait_ge(mixer_const, MIXER_CONST)
            pe.wait_ge(mixer_const_dve, 1)
            pe.wait_ge(mixer_const_act, 1)
            pe.wait_ge(wm_in, 96)

        def pe_mixer(pe):
            def transposes(target, source, n=TT):
                for t in range(n):
                    r = pe.transpose(target[:, t * P:(t + 1) * P], source(t), ident[:, :])
                return r

            def pre(b, q):
                n = SQ * b + q
                pe.wait_ge(zn_ready, n + 1)
                after(pe, softplus_parts, n)
                transposes(pf_uz[1], lambda t: zn[:, t, :]).then_inc(zt_ps_ready, 1)

            def project(target, weights, taps, done):
                for k in range(taps):
                    shift = k if taps > 1 else TAPS - 1
                    r = pe.matmul(target, weights(k), zt[:, shift:shift + BT], start=(k == 0), stop=(k == taps - 1))
                r.then_inc(done, 1)

            def project_u(b, q, k):
                n = SQ * b + q
                pe.wait_ge(zt_ready, 2 * n + 2)
                if k == 0:
                    after(pe, bc_n2_ready, n)
                project(uz_bank(b, q, 0, k), lambda tap: w_tap[:, tap, k * P:(k + 1) * P], TAPS, uz_ps_ready)

            def project_z(b, q, k):
                if not first_block(b, q):
                    pe.wait_ge(silu_u_done, 2 * (SQ * b + q) + k + 1)
                else:
                    pe.wait_ge(residual_done, NB)
                project(uz_bank(b, q, 1, k), lambda tap: w_z[:, k * P:(k + 1) * P], 1, uz_ps_ready)

            def project_bc(b, q):
                if not first_block(b, q):
                    pe.wait_ge(silu_z_done, 2 * (SQ * b + q) + 1)
                project(pf_uz[0][0:2 * DS], lambda tap: w_tap[:, tap, DI:], TAPS, bc_ps_ready)

            def project_dt(b, q):
                if not first_block(b, q):
                    pe.wait_ge(silu_z_done, 2 * (SQ * b + q) + 2)
                else:
                    pe.wait_ge(zt_ready, 2)
                project(pf_uz[1], lambda tap: w_dt, 1, dt_ps_ready)

            def bc_tokens(b, q):
                pe.wait_ge(silu_bc_done, SQ * b + q + 1)
                apart(pe)
                for t in range(TT):
                    r = pe.transpose(pf_uz[0][:, t * 2 * DS:(t + 1) * 2 * DS], bc_act[:, t * P:(t + 1) * P],
                                     ident[0:2 * DS, 0:2 * DS])
                r.then_inc(bct_ps_ready, 1)

            def bc_features(b, q):
                n = SQ * b + q
                pe.wait_ge(bcn_ready, n + 1)
                after(pe, bf_ready, n)
                transposes(pf_b, lambda t: bc_rep[:, 2 * t].rearrange("p r n -> p (r n)"))
                transposes(pf_c, lambda t: bc_rep[:, 2 * t + 1].rearrange("p r n -> p (r n)")).then_inc(rep_ps_ready, 1)

            def token_major(b, q, k):
                n = SQ * b + q
                if k == 0:
                    pe.wait_ge(bf_ready, n + 1)
                    after(pe, silu_g_done, FC * n)
                else:
                    pe.wait_ge(tm_ready, TT * n + k)
                for p in range(2):
                    pe.transpose(pb_t[:, p * P:(p + 1) * P], us[:, q, p, k * P:(k + 1) * P], ident[:, :])
                pe.transpose(pb_t[:, DI:DI + P], bf[:, k, (CT - 1) * P:CT * P], ident[:, :]).then_inc(tm_ps_ready, 1)

            def make_gram(b, q, k):
                n = SQ * b + q
                if k == 0:
                    pe.wait_ge(cfx_ready, NH * n + NH)
                    after(pe, silu_g_done, FC * n)
                else:
                    pe.wait_ge(gram_ready, TT * n + k)
                for j in range(CT):
                    r = pe.matmul(pb_gram[:, j * P:(j + 1) * P], bf[:, k, j * P:(j + 1) * P],
                                  cfx[:, k, j * P:(j + 1) * P], start=True, stop=True)
                r.then_inc(gram_ps_ready, 1)

            def outputs(b, q, k):
                n = SQ * b + q
                tile = TT * n + k
                pe.wait_ge(tm_ready, tile + 1)
                if k == 0:
                    after(pe, hf_ready, FC * n)
                    after(pe, mixer_done, n)
                    pe.wait_ge(cfs_ready, n + 1)
                if k or q:
                    pe.wait_ge(state_ready, tile)
                else:
                    pe.wait_ge(state_clear, b + 1)
                pe.matmul(pb_ds[:, 0:DI], tm[:, k % 2, DI:], tm[:, k % 2, 0:DI], start=True,
                          stop=True).then_inc(ds_ps_ready, 1)
                pe.wait_ge(gram_ready, tile + 1)
                if k == 2:
                    pe.wait_ge(oy_ready, 2 * n + 1)
                for p in range(2):
                    at = slice(p * 2 * P + (k % 2) * P, p * 2 * P + (k % 2 + 1) * P)
                    pe.matmul(pb_o[:, at], state[:, k % 2, p * P:(p + 1) * P], cfs[:, q, k * P:(k + 1) * P],
                              start=True, stop=False)
                    for i in range(2):
                        h = 2 * p + i
                        r = pe.matmul(pb_o[i * DH:(i + 1) * DH, at], tm[:, k % 2, h * DH:(h + 1) * DH],
                                      gram[:, k % 2, :, h, :], start=False, stop=True)
                r.then_inc(o_ps_ready, 1)

            def out_project(b, q):
                n = SQ * b + q
                pe.wait_ge(y_ready, 2 * n + 2)
                pe.wait_ge(state_ready, TT * n + TT)
                for k in range(2):
                    r = pe.matmul(pb_ds, w_out[:, k, :], zs[:, q, k, :], start=(k == 0), stop=(k == 1))
                r.then_inc(mix_f_ps_ready, 1)

            def mix_back(b, q):
                pe.wait_ge(mix_f_ready, SQ * b + q + 1)
                transposes(pb_t, lambda t: mo[:, t * P:(t + 1) * P]).then_inc(mix_ps_ready, 1)

            def h_features(b, q):
                pe.wait_ge(hn_ready, SQ * b + q + 1)
                transposes(pb_t, lambda t: hb[:, t, :]).then_inc(hnt_ps_ready, 1)

            def gate_up(b, q, c):
                n = SQ * b + q
                m = min(P, FF - c * P)
                if c == 0:
                    pe.wait_ge(hnt_ready, n + 1)
                if c == 2:
                    pe.wait_ge(hf_ready, FC * n + 1)
                pe.matmul(pb_gate[c][0:m], w_gate[:, c * P:c * P + m], hnt, start=True, stop=True).then_inc(gate_ps_ready, 1)
                pe.matmul(pb_up[c][0:m], w_up[:, c * P:c * P + m], hnt, start=True, stop=True).then_inc(up_ps_ready, 1)

            def down(b, q):
                n = SQ * b + q
                for c in range(FC):
                    m = min(P, FF - c * P)
                    pe.wait_ge(hf_ready, FC * n + max(c, 1) + 1)
                    r = pe.matmul(pb_down, w_down[0:m, c, :], hf[0:m, c, :], start=(c == 0), stop=(c == FC - 1))
                r.then_inc(ffn_ps_ready, 1)

            def ffn_back(b, q):
                pe.wait_ge(ffn_f_ready, SQ * b + q + 1)
                transposes(pb_o, lambda t: mo[:, t * P:(t + 1) * P]).then_inc(ffn_t_ps_ready, 1)

            def body(now, next, then):
                if now and next:
                    bc_tokens(*next)
                if now:
                    token_major(*now, 1)
                    make_gram(*now, 1)
                    outputs(*now, 0)
                    token_major(*now, 2)
                    make_gram(*now, 2)
                    outputs(*now, 1)
                    token_major(*now, 3)
                    make_gram(*now, 3)
                    outputs(*now, 2)
                if then:
                    pre(*then)
                if now and not next:
                    pe_xt(pe, NB)
                if next:
                    bc_features(*next)
                if then:
                    project_u(*then, 0)
                if now:
                    outputs(*now, 3)
                if now and not next:
                    pe_logits(pe, NB)
                if then:
                    project_u(*then, 1)
                if now:
                    out_project(*now)
                if then:
                    project_z(*then, 0)
                if now:
                    mix_back(*now)
                if now and not next:
                    pe.wait_ge(xt_lo_ready, NB + 1)
                    pe_up(pe, NB, 0)
                if then:
                    project_z(*then, 1)
                    project_bc(*then)
                if now:
                    h_features(*now)
                if then:
                    project_dt(*then)
                if now:
                    gate_up(*now, 0)
                    gate_up(*now, 1)
                if now and not next:
                    pe_gates(pe, NB)
                if now:
                    gate_up(*now, 2)
                    down(*now)
                if next:
                    token_major(*next, 0)
                    make_gram(*next, 0)
                if now:
                    ffn_back(*now)

            def enter(n):
                pre(*n)
                project_dt(*n)
                project_bc(*n)
                project_u(*n, 0)
                bc_tokens(*n)
                project_u(*n, 1)
                project_z(*n, 0)
                project_z(*n, 1)

            in_order(pe, enter, body)

        @block.tensor
        def _(pe):
            pe.wait_ge(pool_const, 3)
            pe.wait_ge(small_in, 32)
            pe_ffn(pe, 0)
            pe_mixer_const(pe)
            pe_mixer(pe)
            pe_ffn(pe, 1)


_OUT_SHAPE = (NSEQ, SEQ, P)


def kernel(**inputs):
    import concourse.bacc as bacc
    from concourse.bass_utils import run_bass_kernel_spmd as run

    arrays = laid_out(inputs)
    nc = bacc.Bacc("TRN2", target_bir_lowering=False, num_devices=1)
    A = {n: nc.dram_tensor("in_" + n, a.shape, mybir.dt.from_np(a.dtype), kind="ExternalInput").ap()
         for n, a in arrays.items()}
    out = nc.dram_tensor("out", _OUT_SHAPE, F32, kind="ExternalOutput").ap()
    macaron(nc, A, out)
    r = run(nc, [{"in_" + n: a for n, a in arrays.items()}], core_ids=[0])
    return r.results[0]["out"]


def laid_out(inputs):
    get = {n: np.ascontiguousarray(a) for n, a in inputs.items()}
    m = {n[8:]: a for n, a in get.items() if n.startswith("L0_attn_")}
    arrays = {n: a for n, a in get.items() if n.startswith("L0_ffn_")}
    arrays["L0_attn_x"] = m["x"]
    arrays["in_proj_t"] = np.ascontiguousarray(m["in_proj_w"].T)
    arrays["out_proj_t"] = np.ascontiguousarray(m["out_proj_w"].T)
    arrays["gate_t"] = np.ascontiguousarray(m["gate_w"].T)
    arrays["up_t"] = np.ascontiguousarray(m["up_w"].T)
    arrays["down_t"] = np.ascontiguousarray(m["down_w"].T)
    arrays["conv_taps"] = np.ascontiguousarray(m["conv_w"].T).reshape(1, TAPS * (DI + 2 * DS))
    col = np.zeros((P, NCOL), np.float32)
    col[:, C_NORM1] = m["norm1_w"]
    col[:, C_NORM2] = m["norm2_w"]
    col[:, C_CONVB:C_CONVB + 2] = m["conv_b"][0:DI].reshape(2, P).T
    col[0:2 * DS, C_CONVBC] = m["conv_b"][DI:]
    col[:, C_ALOG] = np.repeat(m["A_log"][:, None, :], 2, axis=1).reshape(P)
    col[:, C_DTB] = np.repeat(m["dt_bias"], 2 * DS)
    col[:, C_D:C_D + 2] = np.repeat(m["D"], DH).reshape(2, P).T
    part = (np.arange(P) // DS) % 2
    col[:, C_OFFC] = np.where(part == 0, 0.0, 0.25)
    col[:, C_OFFB] = np.where(part == 0, 0.25, 0.5)
    arrays["columns"] = col
    return arrays
```
